# Optimizing a Trainium2 kernel written in Bass

```python
import numpy as np
import jax
import jax.numpy as jnp

def _softmax(x, axis=-1):
    return jax.nn.softmax(x, axis=axis)

def _gelu(x):
    return jax.nn.gelu(x, approximate=True)

def _silu(x):
    return jax.nn.silu(x)

def _sigmoid(x):
    return jax.nn.sigmoid(x)

def _layernorm(x, axis=-1, eps=1e-05):
    m = jnp.mean(x, axis=axis, keepdims=True)
    v = jnp.var(x, axis=axis, keepdims=True)
    return (x - m) / jnp.sqrt(v + eps)

def _scatter_add(tgt, idx, src, axis=0):
    return tgt.at[idx].add(src)

def _segment_sum(src, seg, n):
    return jax.ops.segment_sum(src, seg, n)
kernel_name = 'mk_cond_resid_d4_seqx_r2_e942bf'

def setup_inputs(seed: int=0):
    np.random.seed(seed)
    _w = jnp.asarray

    def _rec_inputs():
        import jax
        import jax.numpy as jnp
        _rk = jax.random.key(seed)
        x = -0.000125 + 0.9999 * jax.random.normal(jax.random.fold_in(_rk, 1), (32, 128, 512), jnp.float32)
        _lenS = 128 - jax.random.randint(jax.random.fold_in(_rk, 7), (32,), 0, max(1, 128 // 4) + 1, jnp.int32)
        _lenS2 = 128 - jax.random.randint(jax.random.fold_in(_rk, 8), (32,), 0, max(1, 128 // 4) + 1, jnp.int32)
        cond_1024 = 0.00513981 + 1.0024 * jax.random.normal(jax.random.fold_in(_rk, 11), (32, 512), jnp.float32)
        return (x, cond_1024)
    x, cond_1024 = _rec_inputs()

    def _L0_cond_setup():
        import jax, jax.numpy as jnp
        import numpy as np
        IN_FEATURES = 512
        OUT_FEATURES = 512
        BATCH = 32
        SEQ = 512
        EPS = 1e-08
        key = jax.random.key(seed)
        k1, k2, k3 = jax.random.split(key, 3)
        Efou = jax.random.normal(k1, (BATCH, SEQ, IN_FEATURES), dtype=jnp.float32)
        y = jax.random.normal(k2, (BATCH, IN_FEATURES), dtype=jnp.float32)
        weight = jax.random.normal(k3, (IN_FEATURES, OUT_FEATURES), dtype=jnp.float32)
        return {'Efou': Efou, 'y': y, 'weight': weight}
    _L0_cond_all = _L0_cond_setup()
    _L0_cond_in = {k: v for k, v in _L0_cond_all.items() if k in ('weight',)}
    del _L0_cond_all

    def _L1_cond_setup():
        import jax, jax.numpy as jnp
        import numpy as np
        N, T, D, H = (64, 256, 512, 512)
        key = jax.random.key(seed)
        k1, k2, k3, k4 = jax.random.split(key, 4)
        x = jax.random.normal(k1, (N, T, D), dtype=jnp.float32)
        h0 = jax.random.normal(k2, (N, H), dtype=jnp.float32)
        Wx = jax.random.normal(k3, (D, H), dtype=jnp.float32) / np.sqrt(D)
        Wh = jax.random.normal(k4, (H, H), dtype=jnp.float32) / np.sqrt(H)
        b = jnp.zeros((H,), dtype=jnp.float32)
        return {'x': x, 'h0': h0, 'Wx': Wx, 'Wh': Wh, 'b': b}
    _L1_cond_all = _L1_cond_setup()
    _L1_cond_in = {k: v for k, v in _L1_cond_all.items() if k in ('Wx', 'Wh', 'b')}
    del _L1_cond_all

    def _L2_cond_setup():
        import jax, jax.numpy as jnp
        import numpy as np
        B, T, D = (128, 32, 512)
        ADA, INTER, RANK = (512, 512, 8)
        LN_EPS = 1e-05

        def _layernorm(x, g, b):
            mu = jnp.mean(x, axis=-1, keepdims=True)
            var = jnp.var(x, axis=-1, keepdims=True)
            return (x - mu) * jax.lax.rsqrt(var + LN_EPS) * g + b
        key = jax.random.key(seed)
        ks = jax.random.split(key, 9)
        return {'x': jax.random.normal(ks[0], (B, T, D), dtype=jnp.float32), 'ada_emb': jax.random.normal(ks[1], (B, ADA), dtype=jnp.float32), 'base_layer': jax.random.normal(ks[2], (D, D), dtype=jnp.float32), 'w1': jax.random.normal(ks[3], (ADA, INTER), dtype=jnp.float32) * 0.02, 'b1': jnp.zeros((INTER,), dtype=jnp.float32), 'w2': jax.random.normal(ks[4], (INTER, 2 * D * RANK), dtype=jnp.float32) * 0.02, 'b2': jnp.zeros((2 * D * RANK,), dtype=jnp.float32), 'ln_g': jnp.ones((ADA,), dtype=jnp.float32), 'ln_b': jnp.zeros((ADA,), dtype=jnp.float32)}
    _L2_cond_all = _L2_cond_setup()
    _L2_cond_in = {k: v for k, v in _L2_cond_all.items() if k in ('base_layer', 'w1', 'b1', 'w2', 'b2', 'ln_g', 'ln_b')}
    del _L2_cond_all

    def _L3_cond_setup():
        import jax, jax.numpy as jnp
        import numpy as np
        import math
        D = 512
        H = 512
        key = jax.random.key(seed)
        k1, k2, k3, k4 = jax.random.split(key, 4)
        x = jax.random.normal(k1, (64, 256, D), dtype=jnp.float32)
        h0 = jax.random.normal(k2, (64, H), dtype=jnp.float32)
        Wx = jax.random.normal(k3, (D, 4 * H), dtype=jnp.float32) / math.sqrt(D)
        Wh = jax.random.normal(k4, (H, 4 * H), dtype=jnp.float32) / math.sqrt(H)
        b = jnp.zeros((4 * H,), dtype=jnp.float32)
        return {'x': x, 'h0': h0, 'Wx': Wx, 'Wh': Wh, 'b': b}
    _L3_cond_all = _L3_cond_setup()
    _L3_cond_in = {k: v for k, v in _L3_cond_all.items() if k in ('Wx', 'Wh', 'b')}
    del _L3_cond_all
    return {'x': x, 'cond_1024': cond_1024, 'L0_cond_weight': _L0_cond_in['weight'], 'L1_cond_Wx': _L1_cond_in['Wx'], 'L1_cond_Wh': _L1_cond_in['Wh'], 'L1_cond_b': _L1_cond_in['b'], 'L2_cond_base_layer': _L2_cond_in['base_layer'], 'L2_cond_w1': _L2_cond_in['w1'], 'L2_cond_b1': _L2_cond_in['b1'], 'L2_cond_w2': _L2_cond_in['w2'], 'L2_cond_b2': _L2_cond_in['b2'], 'L2_cond_ln_g': _L2_cond_in['ln_g'], 'L2_cond_ln_b': _L2_cond_in['ln_b'], 'L3_cond_Wx': _L3_cond_in['Wx'], 'L3_cond_Wh': _L3_cond_in['Wh'], 'L3_cond_b': _L3_cond_in['b']}

def reference(x, cond_1024, L0_cond_weight, L1_cond_Wx, L1_cond_Wh, L1_cond_b, L2_cond_base_layer, L2_cond_w1, L2_cond_b1, L2_cond_w2, L2_cond_b2, L2_cond_ln_g, L2_cond_ln_b, L3_cond_Wx, L3_cond_Wh, L3_cond_b):
    import jax
    import jax.numpy as jnp

    def _L0_cond_ref(Efou, y, weight):
        import jax, jax.numpy as jnp
        import numpy as np
        IN_FEATURES = 512
        OUT_FEATURES = 512
        BATCH = 32
        SEQ = 512
        EPS = 1e-08
        scale = 1.0 / np.sqrt(np.float32(weight.shape[0]))
        ys = y * scale
        d = jax.lax.rsqrt(jnp.einsum('bi,io->bo', ys * ys, weight * weight) + EPS)
        out = jnp.einsum('bsi,io->bso', Efou * ys[:, None, :], weight) * d[:, None, :]
        return out

    def _L1_cond_ref(x, h0, Wx, Wh, b):
        import jax, jax.numpy as jnp
        import numpy as np
        N, T, D, H = (64, 256, 512, 512)
        xW = jnp.einsum('ntd,dh->nth', x, Wx) + b
        xW_t = jnp.swapaxes(xW, 0, 1)

        def step(prev_h, xw):
            next_h = jnp.tanh(prev_h @ Wh + xw)
            return (next_h, next_h)
        _, h_t = jax.lax.scan(step, h0, xW_t)
        return jnp.swapaxes(h_t, 0, 1)

    def _L2_cond_ref(x, ada_emb, base_layer, w1, b1, w2, b2, ln_g, ln_b):
        import jax, jax.numpy as jnp
        import numpy as np
        B, T, D = (128, 32, 512)
        ADA, INTER, RANK = (512, 512, 8)
        LN_EPS = 1e-05

        def _layernorm(x, g, b):
            mu = jnp.mean(x, axis=-1, keepdims=True)
            var = jnp.var(x, axis=-1, keepdims=True)
            return (x - mu) * jax.lax.rsqrt(var + LN_EPS) * g + b
        b, t, d = x.shape
        ae = _layernorm(ada_emb, ln_g, ln_b)
        h = jax.nn.gelu(ae @ w1 + b1, approximate=False)
        xw = h @ w2 + b2
        x_a, x_b = jnp.split(xw, 2, axis=-1)
        x_a = x_a.reshape(b, d, RANK)
        x_b = x_b.reshape(b, d, RANK)
        layer = base_layer[None, :, :] + jnp.einsum('bdr,bkr->bdk', x_a, x_b)
        out = jnp.einsum('btc,bco->bto', x, layer)
        return x + out

    def _L3_cond_ref(x, h0, Wx, Wh, b):
        import jax, jax.numpy as jnp
        import numpy as np
        import math
        D = 512
        H = 512
        Hdim = h0.shape[1]
        xW = jnp.einsum('ntd,dk->ntk', x, Wx) + b
        c0 = jnp.zeros_like(h0)

        def step(carry, xw_t):
            prev_h, prev_c = carry
            a = xw_t + prev_h @ Wh
            i = jax.nn.sigmoid(a[:, :Hdim])
            f = jax.nn.sigmoid(a[:, Hdim:2 * Hdim])
            o = jax.nn.sigmoid(a[:, 2 * Hdim:3 * Hdim])
            g = jnp.tanh(a[:, 3 * Hdim:])
            next_c = f * prev_c + i * g
            next_h = o * jnp.tanh(next_c)
            return ((next_h, next_c), next_h)
        xW_t = jnp.swapaxes(xW, 0, 1)
        _, hs = jax.lax.scan(step, (h0, c0), xW_t)
        hn = jnp.swapaxes(hs, 0, 1)
        return hn
    x = x + _L0_cond_ref(x, cond_1024, L0_cond_weight)
    x = x + _L1_cond_ref(x, cond_1024, L1_cond_Wx, L1_cond_Wh, L1_cond_b)
    x = x + _L2_cond_ref(x, cond_1024, L2_cond_base_layer, L2_cond_w1, L2_cond_b1, L2_cond_w2, L2_cond_b2, L2_cond_ln_g, L2_cond_ln_b)
    x = x + _L3_cond_ref(x, cond_1024, L3_cond_Wx, L3_cond_Wh, L3_cond_b)
    return x

_drawn_inputs = setup_inputs


def setup_inputs(seed=0):
    import zlib

    import numpy as np

    out = dict(_drawn_inputs(seed))
    spreads = {'L1_cond_b': (0.0, 0.1),
     'L2_cond_b1': (0.0, 0.469),
     'L2_cond_b2': (0.0, 0.1),
     'L2_cond_ln_g': (1.0, 0.6),
     'L2_cond_ln_b': (0.0, 0.8),
     'L3_cond_b': (0.0, 0.8)}
    factors = {'L3_cond_Wx': 5.019, 'L3_cond_Wh': 8.0}
    for name, (base, spread) in spreads.items():
        noise = np.random.default_rng([zlib.crc32(name.encode()), seed]).standard_normal(out[name].shape)
        drawn = base * np.exp(spread * noise) if base else spread * noise
        out[name] = jnp.asarray(drawn.astype(out[name].dtype))
    for name, factor in factors.items():
        out[name] = (out[name] * factor).astype(out[name].dtype)
    return out
```

```python
import concourse.bass as bass
from concourse import mybir
from contextlib import ExitStack

B, T, D, H, RANK = 32, 128, 512, 512, 8
P = 128
KC = D // P
STEPS = 4
TOK = STEPS * B
TILES = T // STEPS
GATES = 4
GW = GATES * P
RH = RANK // 2
W2_SLOTS = 4
LN_EPS = 1e-5
L0_EPS = 1e-8


def build(nc, xT, condT, cond, w0, wx1, wh1, b1, base, hw1, hb1, hw2, hb2, ln_g, ln_b, wx3, wh3, b3, out):
    fp32 = mybir.dt.float32
    ALU = mybir.AluOpType
    ACT = mybir.ActivationFunctionType

    ctx = ExitStack()
    with ctx:
        def sb(name, shape, dt=fp32):
            return ctx.enter_context(nc.sbuf_tensor(name, shape, dt))

        def sem(name):
            return ctx.enter_context(nc.semaphore(name))

        def bank(name):
            return ctx.enter_context(nc.psum_tensor(name, [P, 512], fp32))

        w0_sb = sb("w0_sb", [P, KC, D])
        wx1_sb = sb("wx1_sb", [P, KC, H])
        wh1_sb = sb("wh1_sb", [P, KC, H])
        base_sb = sb("base_sb", [P, KC, D])
        wx3_sb = sb("wx3_sb", [P, KC, KC * GW])
        wh3_sb = sb("wh3_sb", [P, KC, KC * GW])
        w2_ring = sb("w2_ring", [P, W2_SLOTS, KC, D])
        w1_sb = w2_ring[:, W2_SLOTS - 1]
        w0_sq = w2_ring[:, W2_SLOTS - 2]
        b1_bc = sb("b1_bc", [P, P])
        b3_bc = sb("b3_bc", [P, GW])
        b2_bc = sb("b2_bc", [P, 4, D])
        a_all = sb("a_all", [P, KC, 2, P])
        b_all = sb("b_all", [P, 2, D])
        a_rows = sb("a_rows", [P, 2, D])
        ident = sb("ident", [P, P])
        same_b = sb("same_b", [P, B])
        condT_sb = sb("condT_sb", [P, KC, B])
        ysT = sb("ysT", [P, KC, B])
        ysq = sb("ysq", [P, KC, B])
        dT = sb("dT", [P, KC, B])
        var_d = sb("var_d", [P, KC, B])
        root_d = sb("root_d", [P, KC, B])
        newton_d = sb("newton_d", [P, KC, B])
        ln_rows = sb("ln_rows", [B, 4, D])
        ae = sb("ae", [B, D])
        hyper = sb("hyper", [B, H])
        aeT = sb("aeT", [P, KC, B])
        hyperT = sb("hyperT", [P, KC, B])
        stats = sb("stats", [B, 6])
        moments = sb("moments", [B, 2])
        ln_s = sb("ln_s", [B, 4])

        xT_sb = [sb(f"xT_sb{q}", [P, KC, STEPS, B]) for q in range(2)]
        xs = sb("xs", [P, KC, STEPS, B])
        l0_out = sb("l0_out", [P, KC, STEPS, B])
        x1T = [sb(f"x1T{q}", [P, KC, STEPS, B]) for q in range(2)]
        x2T = [sb(f"x2T{q}", [P, KC, STEPS, B]) for q in range(2)]
        x3T = [sb(f"x3T{q}", [P, KC, STEPS, B]) for q in range(2)]
        oT = [sb(f"oT{q}", [P, KC, STEPS, B]) for q in range(2)]
        zm = sb("zm", [P, 2, STEPS, B])
        rnn_pre = sb("rnn_pre", [P, P])
        rnn_h = sb("rnn_h", [P, P])
        rnn_hT = sb("rnn_hT", [P, KC, B])
        gates = sb("gates", [P, GW])
        gate_act = sb("gate_act", [P, GW])
        cell = sb("cell", [P, P])
        kept = sb("kept", [P, P])
        added = sb("added", [P, P])
        cell_tanh = sb("cell_tanh", [P, P])
        lstm_h = sb("lstm_h", [P, P])
        lstm_hT = sb("lstm_hT", [P, KC, B])

        ps_l0 = bank("ps_l0")
        ps_rnn = bank("ps_rnn")
        ps_rnn_t = bank("ps_rnn_t")
        ps_z = bank("ps_z")
        ps_x3 = bank("ps_x3")
        ps_gates = [bank("ps_gates0"), bank("ps_gates1")]
        ps_lstm_t = bank("ps_lstm_t")

        ld_cond = sem("ld_cond")
        ld_w0 = sem("ld_w0")
        ld_rnn = sem("ld_rnn")
        ld_w1 = sem("ld_w1")
        ld_base = sem("ld_base")
        ld_b2 = sem("ld_b2")
        ld_lstm = sem("ld_lstm")
        ld_w2 = [sem(f"ld_w2_{n}") for n in range(W2_SLOTS)]
        ld_x = [sem("ld_x0"), sem("ld_x1")]
        st_out = [sem("st_out0"), sem("st_out1")]
        consts_cleared = sem("consts_cleared")
        consts_ready = sem("consts_ready")
        ys_ready = sem("ys_ready")
        dve_set = sem("dve_set")
        dsum_ready = sem("dsum_ready")
        var_ready = sem("var_ready")
        root_ready = sem("root_ready")
        d_ready = sem("d_ready")
        ae_ready = sem("ae_ready")
        aeT_ps = sem("aeT_ps")
        aeT_ready = sem("aeT_ready")
        u_ps = sem("u_ps")
        u_ready = sem("u_ready")
        hyper_ready = sem("hyper_ready")
        hyperT_ps = sem("hyperT_ps")
        hyperT_ready = sem("hyperT_ready")
        w2_used = sem("w2_used")
        rows_ready = sem("rows_ready")
        a_ps = sem("a_ps")
        a_ready = sem("a_ready")
        h0_ready = sem("h0_ready")
        xs_ready = sem("xs_ready")
        l0_ready = sem("l0_ready")
        l0_scaled = sem("l0_scaled")
        x1_ready = sem("x1_ready")
        z_ready = sem("z_ready")
        zm_ready = sem("zm_ready")
        x3_ps = sem("x3_ps")
        x3_ready = sem("x3_ready")
        rnn_ps = sem("rnn_ps")
        rnn_biased = sem("rnn_biased")
        rnn_h_ready = sem("rnn_h_ready")
        rnn_t_ps = sem("rnn_t_ps")
        rnn_hT_ready = sem("rnn_hT_ready")
        x2_ready = sem("x2_ready")
        gates_ps = sem("gates_ps")
        gates_biased = sem("gates_biased")
        gates_acted = sem("gates_acted")
        added_ready = sem("added_ready")
        cell_ready = sem("cell_ready")
        cell_tanh_ready = sem("cell_tanh_ready")
        lstm_h_ready = sem("lstm_h_ready")
        lstm_t_ps = sem("lstm_t_ps")
        lstm_hT_ready = sem("lstm_hT_ready")
        out_ready = sem("out_ready")

        block = ctx.enter_context(nc.Block())

        def stages(i):
            return [0 <= i + k < TILES for k in (1, 0, -1, -2)]

        HEAD = [-1, 0, 1]
        TAIL = [30, 31, 32, 33]

        def pipeline(engine, iteration):
            for i in HEAD:
                iteration(i // 2, i % 2, stages(i), i)
            with engine.Fori(1, 15) as m:
                for p in range(2):
                    iteration(m, p, [True] * 4, None)
            for i in TAIL:
                iteration(i // 2, i % 2, stages(i), i)

        def tile_no(m, p, lag):
            return 2 * m + (p - lag)

        def step_no(m, p, lag, s):
            return 8 * m + (4 * (p - lag) + s)

        def turn(m, p, lag):
            return m + (p - lag) // 2

        def wait(engine, sem_, value):
            if not isinstance(value, int) or value > 0:
                engine.wait_ge(sem_, value)

        @block.sync
        def _(sp):
            sp.dma_start(condT_sb[:], condT).then_inc(ld_cond, 16)
            sp.dma_start(ln_rows[:, 0], cond).then_inc(ld_cond, 16)
            sp.dma_start(ln_rows[:, 1], ln_g.partition_broadcast(B)).then_inc(ld_cond, 16)
            sp.dma_start(ln_rows[:, 2], ln_b.partition_broadcast(B)).then_inc(ld_cond, 16)
            sp.dma_start(ln_rows[:, 3], hb1.partition_broadcast(B)).then_inc(ld_cond, 16)
            sp.dma_start(w0_sb[:], w0.rearrange("(k p) n -> p k n", p=P)).then_inc(ld_w0, 16)
            sp.dma_start(w1_sb, hw1.rearrange("(k p) n -> p k n", p=P)).then_inc(ld_w1, 16)
            for q in range(2):
                sp.dma_start(xT_sb[q][:], xT[q]).then_inc(ld_x[q], 16)
            sp.dma_start(wx1_sb[:], wx1.rearrange("(k p) n -> p k n", p=P)).then_inc(ld_rnn, 16)
            sp.dma_start(wh1_sb[:], wh1.rearrange("(k p) n -> p k n", p=P)).then_inc(ld_rnn, 16)
            for j in range(KC):
                sp.dma_start(b1_bc[B * j:B * j + B], b1[j].partition_broadcast(B)).then_inc(ld_rnn, 16)
                sp.dma_start(b3_bc[B * j:B * j + B], b3[j].partition_broadcast(B)).then_inc(ld_lstm, 16)
            for q in range(4):
                for j in range(RH):
                    sp.dma_start(b2_bc[B * j:B * j + B, q], hb2[q // 2, RH * (q % 2) + j].partition_broadcast(B))\
                      .then_inc(ld_b2, 16)
            for n in range(2 * RANK):
                slot = n % W2_SLOTS
                if slot == W2_SLOTS - 1 and n < W2_SLOTS:
                    sp.wait_ge(u_ps, 1)
                if slot == W2_SLOTS - 2 and n < W2_SLOTS:
                    sp.wait_ge(dsum_ready, 1)
                if n >= W2_SLOTS:
                    sp.wait_ge(w2_used, n - W2_SLOTS + 1)
                sp.dma_start(w2_ring[:, slot], hw2[n // RANK, n % RANK].rearrange("(k p) n -> p k n", p=P))\
                  .then_inc(ld_w2[slot], 16)
            sp.dma_start(base_sb[:], base.rearrange("(k p) n -> p k n", p=P)).then_inc(ld_base, 16)
            sp.dma_start(wx3_sb[:], wx3.rearrange("(k p) n -> p k n", p=P)).then_inc(ld_lstm, 16)
            sp.dma_start(wh3_sb[:], wh3.rearrange("(k p) n -> p k n", p=P)).then_inc(ld_lstm, 16)

            def iteration(m, p, has, i):
                if i is None or 0 <= i + 2 < TILES and i >= 0:
                    wait(sp, x1_ready, tile_no(m, p, 0) + 1)
                    sp.dma_start(xT_sb[p][:], xT[tile_no(m, p, -2)]).then_inc(ld_x[p], 16)
                if has[3]:
                    wait(sp, out_ready, step_no(m, p, 2, STEPS))
                    sp.dma_start(out[tile_no(m, p, 2)], oT[p][:]).then_inc(st_out[p], 16)

            pipeline(sp, iteration)
            for q in range(2):
                sp.wait_ge(st_out[q], 16 * TILES // 2)

        @block.gpsimd
        def _(pool):
            nc.gpsimd.memset(ident[:], 0.0).then_inc(consts_cleared, 1)
            nc.gpsimd.memset(same_b[:], 0.0).then_inc(consts_cleared, 1)
            nc.gpsimd.memset(cell[:], 0.0).then_inc(consts_ready, 1)
            pool.wait_ge(consts_cleared, 2)
            nc.gpsimd.affine_select(out=ident[:], in_=ident[:], compare_op=ALU.not_equal, fill=1.0, base=0,
                                    pattern=[[-1, P]], channel_multiplier=1).then_inc(consts_ready, 1)
            for g in range(RH):
                nc.gpsimd.affine_select(out=same_b[:], in_=same_b[:], compare_op=ALU.not_equal, fill=1.0,
                                        base=-B * g, pattern=[[-1, B]], channel_multiplier=1)\
                  .then_inc(consts_ready, 1)
                pool.wait_ge(consts_ready, 3 + g)
            pool.wait_ge(ys_ready, 1)

            def iteration(m, p, has, i):
                if has[0]:
                    q = (p + 1) % 2
                    wait(pool, ld_x[q], 16 * (turn(m, p, -1) + 1))
                    wait(pool, l0_ready, tile_no(m, p, -1))
                    nc.gpsimd.tensor_tensor(xs[:], xT_sb[q][:], ysT[:].unsqueeze(2).broadcast_to([P, KC, STEPS, B]),
                                            ALU.mult).then_inc(xs_ready, 1)

            pipeline(pool, iteration)

        @block.scalar
        def _(act):
            act.wait_ge(ld_cond, 80)
            nc.scalar.copy(rnn_hT[:], condT_sb[:]).then_inc(h0_ready, 1)
            nc.scalar.copy(lstm_hT[:], condT_sb[:]).then_inc(h0_ready, 1)
            act.wait_ge(var_ready, 2)
            nc.scalar.activation(root_d[:], var_d[:], ACT.Sqrt).then_inc(root_ready, 1)
            nc.scalar.activation(ln_s[:, 1:2], ln_s[:, 0:1], ACT.Sqrt).then_inc(root_ready, 1)
            act.wait_ge(u_ready, 1)
            nc.scalar.activation(hyper[:], ae[:], ACT.Gelu).then_inc(hyper_ready, 1)

            def iteration(m, p, has, i):
                for s in range(STEPS):
                    t, r = step_no(m, p, 2, s), step_no(m, p, 0, s)
                    if has[3]:
                        wait(act, gates_biased, t + 1)
                        nc.scalar.activation(gate_act[:, 0:3 * P], gates[:, 0:3 * P], ACT.Sigmoid).then_inc(gates_acted, 1)
                        nc.scalar.activation(gate_act[:, 3 * P:GW], gates[:, 3 * P:GW], ACT.Tanh).then_inc(gates_acted, 1)
                        wait(act, cell_ready, t + 1)
                        nc.scalar.activation(cell_tanh[:], cell[:], ACT.Tanh).then_inc(cell_tanh_ready, 1)
                    if has[1]:
                        wait(act, rnn_biased, r + 1)
                        nc.scalar.activation(rnn_h[:], rnn_pre[:], ACT.Tanh).then_inc(rnn_h_ready, 1)
                        wait(act, rnn_t_ps, r + 1)
                        wait(act, x2_ready, r)
                        nc.scalar.copy(rnn_hT[:], ps_rnn_t[:, 0:P].rearrange("p (k b) -> p k b", b=B))\
                          .then_inc(rnn_hT_ready, 1)
                    if has[3]:
                        wait(act, lstm_t_ps, t + 1)
                        wait(act, out_ready, t)
                        nc.scalar.copy(lstm_hT[:], ps_lstm_t[:, 0:P].rearrange("p (k b) -> p k b", b=B))\
                          .then_inc(lstm_hT_ready, 1)

            pipeline(act, iteration)

        @block.vector
        def _(dve):
            links = [0]

            def link(ins):
                links[0] += 1
                ins.then_inc(dve_set, 1)
                dve.wait_ge(dve_set, links[0])

            dve.wait_ge(ld_cond, 80)
            nc.vector.tensor_scalar(ysT[:], condT_sb[:], float(D) ** -0.5, None, ALU.mult).then_inc(ys_ready, 1)
            dve.wait_ge(ld_w0, 16)
            nc.vector.tensor_tensor(w0_sq, w0_sb[:], w0_sb[:], ALU.mult)
            dve.wait_ge(ys_ready, 1)
            nc.vector.tensor_tensor(ysq[:], ysT[:], ysT[:], ALU.mult).then_inc(ys_ready, 1)
            link(nc.vector.bn_stats(stats[:], ln_rows[:, 0]))
            link(nc.vector.bn_aggr(moments[:], stats[:]))
            link(nc.vector.tensor_scalar(ln_s[:, 0:1], moments[:, 1:2], LN_EPS, None, ALU.add))
            dve.wait_ge(dsum_ready, 1)
            nc.vector.tensor_scalar(var_d[:], ps_z[:, 0:P].rearrange("p (k b) -> p k b", b=B), L0_EPS, None, ALU.add)\
              .then_inc(var_ready, 2)
            dve.wait_ge(root_ready, 2)
            link(nc.vector.reciprocal(root_d[:], root_d[:]))
            link(nc.vector.tensor_tensor(newton_d[:], root_d[:], root_d[:], ALU.mult))
            link(nc.vector.tensor_tensor(newton_d[:], newton_d[:], var_d[:], ALU.mult))
            link(nc.vector.tensor_scalar(newton_d[:], newton_d[:], -0.5, 1.5, ALU.mult, ALU.add))
            nc.vector.tensor_tensor(dT[:], newton_d[:], root_d[:], ALU.mult).then_inc(d_ready, 1)
            link(nc.vector.reciprocal(ln_s[:, 1:2], ln_s[:, 1:2]))
            link(nc.vector.tensor_tensor(ln_s[:, 2:3], ln_s[:, 1:2], ln_s[:, 1:2], ALU.mult))
            link(nc.vector.tensor_tensor(ln_s[:, 2:3], ln_s[:, 2:3], ln_s[:, 0:1], ALU.mult))
            link(nc.vector.tensor_scalar(ln_s[:, 2:3], ln_s[:, 2:3], -0.5, 1.5, ALU.mult, ALU.add))
            link(nc.vector.tensor_tensor(ln_s[:, 3:4], ln_s[:, 2:3], ln_s[:, 1:2], ALU.mult))
            link(nc.vector.tensor_scalar(ae[:], ln_rows[:, 0], moments[:, 0:1], ln_s[:, 3:4], ALU.subtract, ALU.mult))
            link(nc.vector.tensor_tensor(ae[:], ae[:], ln_rows[:, 1], ALU.mult))
            nc.vector.tensor_tensor(ae[:], ae[:], ln_rows[:, 2], ALU.add).then_inc(ae_ready, 1)
            dve.wait_ge(aeT_ps, 1)
            nc.vector.tensor_copy(aeT[:], ps_rnn_t[:, 0:P].rearrange("p (k b) -> p k b", b=B)).then_inc(aeT_ready, 1)
            dve.wait_ge(u_ps, 1)
            nc.vector.tensor_tensor(ae[:], ps_x3[0:B, :], ln_rows[:, 3], ALU.add).then_inc(u_ready, 1)
            dve.wait_ge(hyperT_ps, 1)
            nc.vector.tensor_copy(hyperT[:], ps_rnn_t[:, 0:P].rearrange("p (k b) -> p k b", b=B)).then_inc(hyperT_ready, 1)
            dve.wait_ge(ld_b2, 16 * 4 * RH)
            for q in range(4):
                dve.wait_ge(w2_used, RH * (q + 1))
                dst = a_rows if q < 2 else b_all
                nc.vector.tensor_tensor(dst[:, q % 2], ps_gates[q % 2][:], b2_bc[:, q], ALU.add).then_inc(rows_ready, 1)
            for half in range(2):
                dve.wait_ge(a_ps, half + 1)
                src = ps_lstm_t if half == 0 else ps_rnn
                nc.vector.tensor_copy(a_all[:, :, half], src[:].rearrange("p (k n) -> p k n", k=KC)).then_inc(a_ready, 1)
            dve.wait_ge(ld_rnn, 96)
            dve.wait_ge(ld_lstm, 96)
            dve.wait_ge(consts_ready, 2 + RH)

            def iteration(m, p, has, i):
                q1 = (p + 1) % 2
                for s in range(STEPS):
                    t, r = step_no(m, p, 2, s), step_no(m, p, 0, s)
                    if has[3]:
                        wait(dve, gates_ps, t + 1)
                        nc.vector.tensor_tensor(gates[:], ps_gates[s % 2][:], b3_bc[:], ALU.add).then_inc(gates_biased, 1)
                        wait(dve, gates_acted, 2 * t + 2)
                        nc.vector.tensor_tensor(kept[:], gate_act[:, P:2 * P], cell[:], ALU.mult)
                        nc.vector.tensor_tensor(added[:], gate_act[:, 0:P], gate_act[:, 3 * P:GW], ALU.mult)\
                          .then_inc(added_ready, 1)
                        wait(dve, added_ready, t + 1)
                        nc.vector.tensor_tensor(cell[:], kept[:], added[:], ALU.add).then_inc(cell_ready, 1)
                    if has[1]:
                        wait(dve, rnn_ps, r + 1)
                        nc.vector.tensor_tensor(rnn_pre[:], ps_rnn[:, 0:P], b1_bc[:], ALU.add).then_inc(rnn_biased, 1)
                    if has[3]:
                        wait(dve, cell_tanh_ready, t + 1)
                        nc.vector.tensor_tensor(lstm_h[:], gate_act[:, 2 * P:3 * P], cell_tanh[:], ALU.mult)\
                          .then_inc(lstm_h_ready, 1)
                    if has[1]:
                        wait(dve, rnn_hT_ready, r + 1)
                        nc.vector.tensor_tensor(x2T[p][:, :, s], x1T[p][:, :, s], rnn_hT[:], ALU.add).then_inc(x2_ready, 1)
                    if has[3]:
                        wait(dve, lstm_hT_ready, t + 1)
                        if s == 0:
                            wait(dve, st_out[p], 16 * turn(m, p, 2))
                        nc.vector.tensor_tensor(oT[p][:, :, s], x3T[p][:, :, s], lstm_hT[:], ALU.add).then_inc(out_ready, 1)
                    if has[2] and s == 0:
                        a = tile_no(m, p, 1)
                        wait(dve, z_ready, a + 1)
                        nc.vector.tensor_tensor(zm[:].rearrange("p h t b -> p (h t) b"),
                                                ps_z[:, 0:2 * P].rearrange("p (n b) -> p n b", b=B),
                                                same_b[:].unsqueeze(1).broadcast_to([P, 2 * STEPS, B]), ALU.mult)\
                          .then_inc(zm_ready, 1)
                    if has[2] and s == 2:
                        a = tile_no(m, p, 1)
                        wait(dve, x3_ps, a + 1)
                        nc.vector.scalar_tensor_tensor(x3T[q1][:].rearrange("p k t b -> p (k t b)"),
                                                       x2T[q1][:].rearrange("p k t b -> p (k t b)"), 2.0, ps_x3[:],
                                                       ALU.mult, ALU.add).then_inc(x3_ready, 1)
                    if has[0] and s == 3:
                        a = tile_no(m, p, -1)
                        wait(dve, l0_ready, a + 1)
                        nc.vector.tensor_tensor(l0_out[:], ps_l0[:].rearrange("p (k t b) -> p k t b", t=STEPS, b=B),
                                                dT[:].unsqueeze(2).broadcast_to([P, KC, STEPS, B]), ALU.mult)\
                          .then_inc(l0_scaled, 1)
                        wait(dve, l0_scaled, a + 1)
                        nc.vector.tensor_tensor(x1T[q1][:], l0_out[:], xT_sb[q1][:], ALU.add).then_inc(x1_ready, 1)

            pipeline(dve, iteration)

        @block.tensor
        def _(pe):
            pe.wait_ge(ys_ready, 2)
            for oc in range(KC):
                for k in range(KC):
                    last = nc.tensor.matmul(ps_z[:, B * oc:B * oc + B], w0_sq[:, k, P * oc:P * oc + P], ysq[:, k],
                                            start=(k == 0), stop=(k == KC - 1))
            last.then_inc(dsum_ready, 1)
            pe.wait_ge(consts_ready, 2 + RH)
            pe.wait_ge(ae_ready, 1)
            for k in range(KC):
                last = nc.tensor.transpose(ps_rnn_t[:, B * k:B * k + B], ae[:, P * k:P * k + P], ident[0:B, 0:B])
            last.then_inc(aeT_ps, 1)
            pe.wait_ge(ld_w1, 16)
            pe.wait_ge(aeT_ready, 1)
            for k in range(KC):
                last = nc.tensor.matmul(ps_x3[0:B, :], aeT[:, k], w1_sb[:, k], start=(k == 0), stop=(k == KC - 1))
            last.then_inc(u_ps, 1)
            pe.wait_ge(hyper_ready, 1)
            for k in range(KC):
                last = nc.tensor.transpose(ps_rnn_t[:, B * k:B * k + B], hyper[:, P * k:P * k + P], ident[0:B, 0:B])
            last.then_inc(hyperT_ps, 1)
            pe.wait_ge(hyperT_ready, 1)
            for n in range(2 * RANK):
                q, j = n // RH, n % RH
                if q >= 2 and j == 0:
                    pe.wait_ge(rows_ready, q - 1)
                pe.wait_ge(ld_w2[n % W2_SLOTS], 16 * (n // W2_SLOTS + 1))
                for k in range(KC):
                    last = nc.tensor.matmul(ps_gates[q % 2][B * j:B * j + B, :], hyperT[:, k], w2_ring[:, n % W2_SLOTS, k],
                                            start=(k == 0), stop=(k == KC - 1), tile_position=(0, B * j))
                last.then_inc(w2_used, 1)
            for half in range(2):
                pe.wait_ge(rows_ready, half + 1)
                dst = ps_lstm_t if half == 0 else ps_rnn
                for k in range(KC):
                    last = nc.tensor.transpose(dst[:, P * k:P * k + P], a_rows[:, half, P * k:P * k + P], ident[:])
                last.then_inc(a_ps, 1)
            pe.wait_ge(rows_ready, 4)
            pe.wait_ge(a_ready, 2)
            pe.wait_ge(h0_ready, 2)
            pe.wait_ge(ld_rnn, 96)
            pe.wait_ge(ld_base, 16)
            pe.wait_ge(ld_lstm, 96)

            def l0_chunks(q, chunks):
                for oc in chunks:
                    for k in range(KC):
                        last = nc.tensor.matmul(ps_l0[:, TOK * oc:TOK * oc + TOK], w0_sb[:, k, P * oc:P * oc + P],
                                                xs[:, k], start=(k == 0), stop=(k == KC - 1))
                return last

            def x3_chunks(q, chunks):
                for oc in chunks:
                    for k in range(KC):
                        nc.tensor.matmul(ps_x3[:, TOK * oc:TOK * oc + TOK], base_sb[:, k, P * oc:P * oc + P],
                                         x2T[q][:, k], start=(k == 0), stop=False)
                    for half in range(2):
                        last = nc.tensor.matmul(ps_x3[:, TOK * oc:TOK * oc + TOK], b_all[:, half, P * oc:P * oc + P],
                                                zm[:, half], start=False, stop=(half == 1))
                return last

            def gate_product(bank_, lhsT, w, start, stop):
                for k in range(KC):
                    for j in range(KC):
                        last = nc.tensor.matmul(bank_[B * j:B * j + B, :], lhsT[:, k], w[:, k, GW * j:GW * j + GW],
                                                start=(start and k == 0), stop=(stop and k == KC - 1),
                                                tile_position=(0, B * j))
                return last

            def rnn_product(lhsT, w, start, stop):
                for k in range(KC):
                    for j in range(KC):
                        last = nc.tensor.matmul(ps_rnn[B * j:B * j + B, 0:P], lhsT[:, k], w[:, k, P * j:P * j + P],
                                                start=(start and k == 0), stop=(stop and k == KC - 1),
                                                tile_position=(0, B * j))
                return last

            def iteration(m, p, has, i):
                q1 = (p + 1) % 2
                for s in range(STEPS):
                    t, r = step_no(m, p, 2, s), step_no(m, p, 0, s)
                    if has[3]:
                        wait(pe, lstm_hT_ready, t)
                        gate_product(ps_gates[s % 2], lstm_hT, wh3_sb, False, True).then_inc(gates_ps, 1)
                    if has[1]:
                        if s == 0:
                            wait(pe, x1_ready, tile_no(m, p, 0) + 1)
                        rnn_product(x1T[p][:, :, s], wx1_sb, True, False)
                        wait(pe, rnn_hT_ready, r)
                        rnn_product(rnn_hT, wh1_sb, False, True).then_inc(rnn_ps, 1)
                    if s < STEPS - 1 and has[3]:
                        gate_product(ps_gates[(s + 1) % 2], x3T[p][:, :, s + 1], wx3_sb, True, False)
                    if s == STEPS - 1 and has[2]:
                        wait(pe, x3_ready, tile_no(m, p, 1) + 1)
                        gate_product(ps_gates[(s + 1) % 2], x3T[q1][:, :, 0], wx3_sb, True, False)
                    if has[1]:
                        wait(pe, rnn_h_ready, r + 1)
                        nc.tensor.transpose(ps_rnn_t[:, 0:P], rnn_h[:], ident[:]).then_inc(rnn_t_ps, 1)
                    if has[3]:
                        wait(pe, lstm_h_ready, t + 1)
                        nc.tensor.transpose(ps_lstm_t[:, 0:P], lstm_h[:], ident[:]).then_inc(lstm_t_ps, 1)
                    if has[2] and s == 0:
                        wait(pe, x2_ready, step_no(m, p, 1, STEPS))
                        for half in range(2):
                            for k in range(KC):
                                last = nc.tensor.matmul(ps_z[:, P * half:P * half + P], a_all[:, k, half], x2T[q1][:, k],
                                                        start=(k == 0), stop=(k == KC - 1))
                        last.then_inc(z_ready, 1)
                    if has[0] and s == 0:
                        wait(pe, xs_ready, tile_no(m, p, -1) + 1)
                        l0_chunks(q1, (0, 1))
                    if has[2] and s == 1:
                        wait(pe, zm_ready, tile_no(m, p, 1) + 1)
                        x3_chunks(q1, (0, 1))
                    if has[2] and s == 2:
                        x3_chunks(q1, (2, 3)).then_inc(x3_ps, 1)
                    if has[0] and s == 3:
                        l0_chunks(q1, (2, 3)).then_inc(l0_ready, 1)

            pipeline(pe, iteration)


def kernel(**inputs):
    import numpy as np
    import concourse.bacc as bacc
    from concourse.bass_utils import run_bass_kernel_spmd

    a = {k: np.asarray(v) for k, v in inputs.items()}
    feature_major = (TILES, STEPS, B, KC, P)

    def gates_by_chunk(w):
        return w.reshape(-1, GATES, KC, P).transpose(0, 2, 1, 3).reshape(w.shape[0] if w.ndim > 1 else KC, -1)

    arrays = {
        "xT": a["x"].transpose(1, 0, 2).reshape(feature_major).transpose(0, 4, 3, 1, 2),
        "condT": a["cond_1024"].reshape(B, KC, P).transpose(2, 1, 0),
        "cond": a["cond_1024"],
        "w0": a["L0_cond_weight"],
        "wx1": a["L1_cond_Wx"], "wh1": a["L1_cond_Wh"], "b1": a["L1_cond_b"].reshape(KC, P),
        "base": a["L2_cond_base_layer"],
        "hw1": a["L2_cond_w1"], "hb1": a["L2_cond_b1"],
        "hw2": a["L2_cond_w2"].reshape(-1, 2, D, RANK).transpose(1, 3, 0, 2),
        "hb2": a["L2_cond_b2"].reshape(2, D, RANK).transpose(0, 2, 1),
        "ln_g": a["L2_cond_ln_g"], "ln_b": a["L2_cond_ln_b"],
        "wx3": gates_by_chunk(a["L3_cond_Wx"]), "wh3": gates_by_chunk(a["L3_cond_Wh"]),
        "b3": gates_by_chunk(a["L3_cond_b"]),
    }
    nc = bacc.Bacc("TRN2", target_bir_lowering=False, num_devices=1)
    fed, args = {}, []
    for name, v in arrays.items():
        v = np.ascontiguousarray(v)
        fed[f"in_{name}"] = v
        args.append(nc.dram_tensor(f"in_{name}", v.shape, mybir.dt.from_np(v.dtype), kind="ExternalInput").ap())
    out = nc.dram_tensor("outT", (TILES, P, KC, STEPS, B), mybir.dt.float32, kind="ExternalOutput").ap()
    build(nc, *args, out)
    r = run_bass_kernel_spmd(nc, [fed], core_ids=[0])
    got = r.results[0]["outT"]
    return got.transpose(4, 0, 3, 2, 1).reshape(B, T, D)
```

```python
import concourse.bass as bass
from concourse import mybir
from contextlib import ExitStack

B, T, D, H, RANK = 32, 128, 512, 512, 8
P = 128
KC = D // P
STEPS = 4
TOK = STEPS * B
TILES = T // STEPS
GATES = 4
GW = GATES * P
RH = RANK // 2
RING = 4
MOVES = 16 * STEPS * KC
LN_EPS = 1e-5
L0_EPS = 1e-8


def build(nc, xT, condT, cond, w0, wx1, wh1, b1T, base, hw1, hb1, hw2, hb2, ln_g, ln_b, wx3, wh3, b3, out):
    fp32 = mybir.dt.float32
    f32r = mybir.dt.float32r
    fp16 = mybir.dt.float16
    i32 = mybir.dt.int32
    ALU = mybir.AluOpType
    ACT = mybir.ActivationFunctionType
    AX = mybir.AxisListType

    ctx = ExitStack()
    with ctx:
        def sb(name, shape, dt=fp32):
            return ctx.enter_context(nc.sbuf_tensor(name, shape, dt))

        def sem(name):
            return ctx.enter_context(nc.semaphore(name))

        def bank(name):
            return ctx.enter_context(nc.psum_tensor(name, [P, 512], fp32))

        w0_sb = sb("w0_sb", [P, KC, D])
        wx1_sb = sb("wx1_sb", [P, KC, H])
        wh1_staged = wx1_sb
        wh1_hi = sb("wh1_hi", [P, KC, H], fp16)
        wh1_lo = sb("wh1_lo", [P, KC, H], fp16)
        base_sb = sb("base_sb", [P, KC, D])
        w0_sq = base_sb
        wx3_hi = sb("wx3_hi", [P, KC, KC * GW], f32r)
        wx3_lo = sb("wx3_lo", [P, KC, KC * GW], f32r)
        wh3_hi = sb("wh3_hi", [P, KC, KC * GW], fp16)
        wh3_lo = sb("wh3_lo", [P, KC, KC * GW], fp16)
        b1T_sb = sb("b1T_sb", [P, KC])
        b3_bc = sb("b3_bc", [P, KC * GW])
        b2_bc = b3_bc[:].rearrange("p (q n) -> p q n", q=4)
        w1_sb = b3_bc[:].rearrange("p (k n) -> p k n", k=KC)
        a_all = sb("a_all", [P, KC, 2, P])
        b_all = sb("b_all", [P, 2, D])
        ident = sb("ident", [P, P])
        ones = sb("ones", [4, P])
        same_b = sb("same_b", [P, B])
        condT_sb = sb("condT_sb", [P, KC, B])
        ysT = sb("ysT", [P, KC, B])
        ysq = sb("ysq", [P, KC, B])
        dT = sb("dT", [P, KC, B])
        early = sb("early", [P, 4, KC, STEPS, B])
        rows = early[:].rearrange("p n k t b -> p n (k t b)")
        ln_rows = rows[0:B]
        ae, hyper = ln_rows[:, 0], ln_rows[:, 1]
        a_rows = rows[:, 0:2]
        x1T = [early[:, q] for q in range(2)]
        x2T = [early[:, 2 + q] for q in range(2)]
        aeT = sb("aeT", [P, KC, B])
        hyperT = sb("hyperT", [P, KC, B])
        stats = sb("stats", [B, 6])
        moments = sb("moments", [B, 2])
        ln_s = sb("ln_s", [B, 4])
        absmax = sb("absmax", [P, 4])
        absmax_all = sb("absmax_all", [4, 1])
        absmax_diag = sb("absmax_diag", [4, 4])
        scales = sb("scales", [P, 4])
        unscales = sb("unscales", [P, 4])
        s_h, s_wh1, s_wh3 = (scales[:, n:n + 1] for n in range(3))
        un_rnn, un_lstm = (unscales[:, n:n + 1] for n in (1, 2))

        shared = sb("shared", [P, RING, KC * D])
        ring = shared[:].rearrange("p r (k n) -> p r k n", k=KC)
        xw_step = [shared[:, q].rearrange("p (t n) -> p t n", t=STEPS) for q in range(2)]
        xw_tok = shared[:, 2].rearrange("p (j n) -> p j n", j=KC)
        late = shared[:, 3].rearrange("p (n k t b) -> p n k t b", n=4, k=KC, t=STEPS)
        x3T = [late[:, q] for q in range(2)]
        xs = late[:, 2]
        xw1T = late[:, 3]
        xT_sb = [sb(f"xT_sb{q}", [P, KC, STEPS, B]) for q in range(2)]
        x3_hi = sb("x3_hi", [P, KC, TOK], f32r)
        x3_lo = sb("x3_lo", [P, KC, TOK], f32r)
        zm = sb("zm", [P, 2, STEPS, B])
        rnn_half = sb("rnn_half", [P, KC, B])
        rnn_pre = sb("rnn_pre", [P, KC, B])
        rnn_h = sb("rnn_h", [P, KC, B])
        rnn_h16 = sb("rnn_h16", [P, KC, 2, B], fp16)
        gates = sb("gates", [P, GW])
        gate_act = sb("gate_act", [P, GW])
        var_d, root_d, newton_d = (gate_act[:, P * n:P * n + P].rearrange("p (k b) -> p k b", b=B) for n in range(3))
        cell = sb("cell", [P, P])
        kept = sb("kept", [P, P])
        added = sb("added", [P, P])
        cell_tanh = sb("cell_tanh", [P, P])
        lstm_h = sb("lstm_h", [P, P])
        lstm_h16 = sb("lstm_h16", [P, 2, KC, B], fp16)

        ps_feat = bank("ps_feat")
        ps_rnn = bank("ps_rnn")
        ps_z = bank("ps_z")
        ps_x3 = bank("ps_x3")
        ps_xw = [bank("ps_xw0"), bank("ps_xw1")]
        ps_gates = bank("ps_gates")
        ps_lstm_t = bank("ps_lstm_t")

        ld_cond = sem("ld_cond")
        ld_w0 = sem("ld_w0")
        ld_rnn = sem("ld_rnn")
        ld_w1 = sem("ld_w1")
        ld_wh1 = sem("ld_wh1")
        ld_base = sem("ld_base")
        ld_b2 = sem("ld_b2")
        ld_b3 = sem("ld_b3")
        ld_ring = [sem(f"ld_ring{n}") for n in range(RING)]
        ld_x = [sem("ld_x0"), sem("ld_x1")]
        xw_moved = [sem("xw_moved0"), sem("xw_moved1")]
        st_out = [sem("st_out0"), sem("st_out1")]
        consts_cleared = sem("consts_cleared")
        consts_ready = sem("consts_ready")
        ys_ready = sem("ys_ready")
        dve_set = sem("dve_set")
        dsum_ready = sem("dsum_ready")
        var_ready = sem("var_ready")
        root_ready = sem("root_ready")
        d_ready = sem("d_ready")
        ae_ready = sem("ae_ready")
        aeT_ps = sem("aeT_ps")
        aeT_ready = sem("aeT_ready")
        u_ps = sem("u_ps")
        u_ready = sem("u_ready")
        hyper_ready = sem("hyper_ready")
        hyperT_ps = sem("hyperT_ps")
        hyperT_ready = sem("hyperT_ready")
        absmax_ready = sem("absmax_ready")
        absmax_ps = sem("absmax_ps")
        diag_ready = sem("diag_ready")
        spread_ps = sem("spread_ps")
        scales_ready = sem("scales_ready")
        hi_ready = sem("hi_ready")
        split_ready = sem("split_ready")
        wx3_ready = sem("wx3_ready")
        w2_used = sem("w2_used")
        rows_ready = sem("rows_ready")
        a_ps = sem("a_ps")
        a_ready = sem("a_ready")
        xs_ready = sem("xs_ready")
        l0_ready = sem("l0_ready")
        l0_scaled = sem("l0_scaled")
        x1_ready = sem("x1_ready")
        xw1_ps = sem("xw1_ps")
        xw1_ready = sem("xw1_ready")
        z_ready = sem("z_ready")
        zm_ready = sem("zm_ready")
        x3_ps = sem("x3_ps")
        x3_ready = sem("x3_ready")
        x3_hi_ready = sem("x3_hi_ready")
        x3_lo_ready = sem("x3_lo_ready")
        xw_ps = sem("xw_ps")
        xw_ready = sem("xw_ready")
        rnn_ps = sem("rnn_ps")
        rnn_half_ready = sem("rnn_half_ready")
        rnn_pre_ready = sem("rnn_pre_ready")
        rnn_h_ready = sem("rnn_h_ready")
        rnn_hi_ready = sem("rnn_hi_ready")
        rnn_lo_ready = sem("rnn_lo_ready")
        x2_ready = sem("x2_ready")
        gates_ps = sem("gates_ps")
        gates_ready = sem("gates_ready")
        gates_acted = sem("gates_acted")
        added_ready = sem("added_ready")
        cell_ready = sem("cell_ready")
        cell_tanh_ready = sem("cell_tanh_ready")
        lstm_h_ready = sem("lstm_h_ready")
        lstm_t_ps = sem("lstm_t_ps")
        lstm_hi_ready = sem("lstm_hi_ready")
        lstm_lo_ready = sem("lstm_lo_ready")
        out_ready = sem("out_ready")

        block = ctx.enter_context(nc.Block())

        STAGED_WH3, STAGED_W2, STAGED_WX3 = 0, KC, KC + 2 * RANK
        STAGED = STAGED_WX3 + KC

        def staged(n):
            return n % RING, 16 * (n // RING + 1)

        def stages(i):
            return [0 <= i + k < TILES for k in (1, 0, -1, -2)]

        HEAD = [-1, 0, 1]
        TAIL = [30, 31, 32, 33]

        def pipeline(engine, iteration):
            for i in HEAD:
                iteration(i // 2, i % 2, stages(i), i)
            with engine.Fori(1, 15) as m:
                for p in range(2):
                    iteration(m, p, [True] * 4, None)
            for i in TAIL:
                iteration(i // 2, i % 2, stages(i), i)

        def tile_no(m, p, lag):
            return 2 * m + (p - lag)

        def step_no(m, p, lag, s):
            return 8 * m + (4 * (p - lag) + s)

        def turn(m, p, lag):
            return m + (p - lag) // 2

        def wait(engine, sem_, value):
            if not isinstance(value, int) or value > 0:
                engine.wait_ge(sem_, value)

        @block.sync
        def _(sp):
            sp.dma_start(condT_sb[:], condT).then_inc(ld_cond, 16)
            sp.dma_start(ln_rows[:, 0], cond).then_inc(ld_cond, 16)
            sp.dma_start(ln_rows[:, 1], ln_g.partition_broadcast(B)).then_inc(ld_cond, 16)
            sp.dma_start(ln_rows[:, 2], ln_b.partition_broadcast(B)).then_inc(ld_cond, 16)
            sp.dma_start(ln_rows[:, 3], hb1.partition_broadcast(B)).then_inc(ld_cond, 16)
            sp.dma_start(w0_sb[:], w0.rearrange("(k p) n -> p k n", p=P)).then_inc(ld_w0, 16)
            sp.dma_start(w1_sb, hw1.rearrange("(k p) n -> p k n", p=P)).then_inc(ld_w1, 16)
            sp.dma_start(wh1_staged[:], wh1.rearrange("(k p) n -> p k n", p=P)).then_inc(ld_wh1, 16)
            for q in range(2):
                sp.dma_start(xT_sb[q][:], xT[q]).then_inc(ld_x[q], 16)
            for n in range(STAGED):
                slot, _ = staged(n)
                if n == STAGED_W2:
                    sp.wait_ge(u_ps, 1)
                    for q in range(4):
                        for j in range(RH):
                            sp.dma_start(b2_bc[B * j:B * j + B, q],
                                         hb2[q // 2, RH * (q % 2) + j].partition_broadcast(B)).then_inc(ld_b2, 16)
                if STAGED_W2 <= n < STAGED_W2 + KC:
                    sp.wait_ge(split_ready, 3 + n - STAGED_W2 + 1)
                if n >= STAGED_W2 + KC:
                    sp.wait_ge(w2_used, n - STAGED_W2 - KC + 1)
                if n < STAGED_W2:
                    src = wh3[P * (n - STAGED_WH3):P * (n - STAGED_WH3 + 1)].rearrange("p (k n) -> p k n", k=KC)
                elif n < STAGED_WX3:
                    r = n - STAGED_W2
                    src = hw2[r // RANK, r % RANK].rearrange("(k p) n -> p k n", p=P)
                else:
                    src = wx3[P * (n - STAGED_WX3):P * (n - STAGED_WX3 + 1)].rearrange("p (k n) -> p k n", k=KC)
                sp.dma_start(ring[:, slot], src).then_inc(ld_ring[slot], 16)
            sp.wait_ge(split_ready, 3)
            sp.dma_start(wx1_sb[:], wx1.rearrange("(k p) n -> p k n", p=P)).then_inc(ld_rnn, 16)
            sp.dma_start(b1T_sb[:], b1T).then_inc(ld_rnn, 16)
            sp.wait_ge(dsum_ready, 1)
            sp.dma_start(base_sb[:], base.rearrange("(k p) n -> p k n", p=P)).then_inc(ld_base, 16)
            sp.wait_ge(rows_ready, 4)
            sp.dma_start(b3_bc[:], b3.partition_broadcast(P)).then_inc(ld_b3, 16)

            def iteration(m, p, has, i):
                q1 = (p + 1) % 2
                if i is None or 0 <= i + 2 < TILES and i >= 0:
                    wait(sp, x1_ready, tile_no(m, p, 0) + 1)
                    sp.dma_start(xT_sb[p][:], xT[tile_no(m, p, -2)]).then_inc(ld_x[p], 16)
                if has[2]:
                    for j in range(KC):
                        wait(sp, xw_ready, step_no(m, p, 1, j + 1))
                        for s in range(STEPS):
                            sp.dma_start(xw_step[q1][B * j:B * j + B, s], xw_tok[B * s:B * s + B, j])\
                              .then_inc(xw_moved[q1], 16)
                if has[3]:
                    wait(sp, out_ready, step_no(m, p, 2, STEPS))
                    sp.dma_start(out[tile_no(m, p, 2)], x3T[p]).then_inc(st_out[p], 16)

            pipeline(sp, iteration)
            for q in range(2):
                sp.wait_ge(st_out[q], 16 * TILES // 2)

        @block.gpsimd
        def _(pool):
            nc.gpsimd.memset(ident[:], 0.0).then_inc(consts_cleared, 1)
            nc.gpsimd.memset(same_b[:], 0.0).then_inc(consts_cleared, 1)
            nc.gpsimd.memset(cell[:], 0.0).then_inc(consts_ready, 1)
            nc.gpsimd.memset(ones[:], 1.0).then_inc(consts_ready, 1)
            pool.wait_ge(consts_cleared, 2)
            nc.gpsimd.affine_select(out=ident[:], in_=ident[:], compare_op=ALU.not_equal, fill=1.0, base=0,
                                    pattern=[[-1, P]], channel_multiplier=1).then_inc(consts_ready, 1)
            for g in range(RH):
                nc.gpsimd.affine_select(out=same_b[:], in_=same_b[:], compare_op=ALU.not_equal, fill=1.0,
                                        base=-B * g, pattern=[[-1, B]], channel_multiplier=1)\
                  .then_inc(consts_ready, 1)
                pool.wait_ge(consts_ready, 4 + g)
            for k in range(KC):
                slot, landed = staged(STAGED_WX3 + k)
                pool.wait_ge(ld_ring[slot], landed)
                pool.wait_ge(hi_ready, 3 + KC + k + 1)
                nc.gpsimd.tensor_tensor(wx3_lo[:, k], shared[:, slot], wx3_hi[:, k].bitcast(fp32), ALU.subtract)\
                  .then_inc(wx3_ready, 1)
            pool.wait_ge(ys_ready, 1)
            pool.wait_ge(wx3_ready, KC)

            def iteration(m, p, has, i):
                q1 = (p + 1) % 2
                if has[0]:
                    wait(pool, ld_x[q1], 16 * (turn(m, p, -1) + 1))
                    wait(pool, l0_ready, tile_no(m, p, -1))
                    nc.gpsimd.tensor_tensor(xs, xT_sb[q1][:], ysT[:].unsqueeze(2).broadcast_to([P, KC, STEPS, B]),
                                            ALU.mult).then_inc(xs_ready, 1)
                if has[2]:
                    a = tile_no(m, p, 1)
                    wait(pool, x3_hi_ready, a + 1)
                    nc.gpsimd.tensor_tensor(x3_lo[:], x3T[q1].rearrange("p k t b -> p k (t b)"),
                                            x3_hi[:].bitcast(fp32), ALU.subtract).then_inc(x3_lo_ready, 1)

            pipeline(pool, iteration)

        @block.scalar
        def _(act):
            act.wait_ge(var_ready, 2)
            nc.scalar.activation(root_d, var_d, ACT.Sqrt).then_inc(root_ready, 1)
            nc.scalar.activation(ln_s[:, 1:2], ln_s[:, 0:1], ACT.Sqrt).then_inc(root_ready, 1)
            act.wait_ge(u_ready, 1)
            nc.scalar.activation(hyper, ae, ACT.Gelu).then_inc(hyper_ready, 1)
            act.wait_ge(scales_ready, 2)
            nc.scalar.activation(rnn_h16[:, :, 0], condT_sb[:], ACT.Copy, scale=s_h).then_inc(hi_ready, 1)
            nc.scalar.activation(lstm_h16[:, 0], condT_sb[:], ACT.Copy, scale=s_h).then_inc(hi_ready, 1)
            act.wait_ge(ld_wh1, 16)
            nc.scalar.activation(wh1_hi[:], wh1_staged[:], ACT.Copy, scale=s_wh1).then_inc(hi_ready, 1)
            for k in range(KC):
                slot, landed = staged(STAGED_WH3 + k)
                act.wait_ge(ld_ring[slot], landed)
                nc.scalar.activation(wh3_hi[:, k], shared[:, slot], ACT.Copy, scale=s_wh3).then_inc(hi_ready, 1)
            for k in range(KC):
                slot, landed = staged(STAGED_WX3 + k)
                act.wait_ge(ld_ring[slot], landed)
                nc.scalar.copy(wx3_hi[:, k], shared[:, slot]).then_inc(hi_ready, 1)

            def iteration(m, p, has, i):
                q1 = (p + 1) % 2
                for s in range(STEPS):
                    t, r = step_no(m, p, 2, s), step_no(m, p, 0, s)
                    if has[3]:
                        wait(act, gates_ready, t + 1)
                        nc.scalar.activation(gate_act[:, 0:3 * P], gates[:, 0:3 * P], ACT.Sigmoid).then_inc(gates_acted, 1)
                        nc.scalar.activation(gate_act[:, 3 * P:GW], gates[:, 3 * P:GW], ACT.Tanh).then_inc(gates_acted, 1)
                    if has[1]:
                        wait(act, rnn_pre_ready, r + 1)
                        wait(act, x2_ready, r)
                        nc.scalar.activation(rnn_h[:], rnn_pre[:], ACT.Tanh).then_inc(rnn_h_ready, 1)
                        wait(act, rnn_h_ready, r + 1)
                        nc.scalar.activation(rnn_h16[:, :, 0], rnn_h[:], ACT.Copy, scale=s_h).then_inc(rnn_hi_ready, 1)
                    if has[3]:
                        wait(act, cell_ready, t + 1)
                        nc.scalar.activation(cell_tanh[:], cell[:], ACT.Tanh).then_inc(cell_tanh_ready, 1)
                        wait(act, lstm_t_ps, t + 1)
                        nc.scalar.activation(lstm_h16[:, 0], ps_lstm_t[:, 0:P].rearrange("p (k b) -> p k b", b=B),
                                             ACT.Copy, scale=s_h).then_inc(lstm_hi_ready, 1)
                    if has[2] and s == 1:
                        a = tile_no(m, p, 1)
                        wait(act, x3_ready, a + 1)
                        nc.scalar.copy(x3_hi[:], x3T[q1].rearrange("p k t b -> p k (t b)")).then_inc(x3_hi_ready, 1)

            pipeline(act, iteration)

        @block.vector
        def _(dve):
            links = [0]

            def link(ins):
                links[0] += 1
                ins.then_inc(dve_set, 1)
                dve.wait_ge(dve_set, links[0])

            dve.wait_ge(ld_cond, 80)
            nc.vector.tensor_scalar(ysT[:], condT_sb[:], float(D) ** -0.5, None, ALU.mult).then_inc(ys_ready, 1)
            dve.wait_ge(ld_w0, 16)
            nc.vector.tensor_tensor(w0_sq[:], w0_sb[:], w0_sb[:], ALU.mult)
            dve.wait_ge(ys_ready, 1)
            nc.vector.tensor_tensor(ysq[:], ysT[:], ysT[:], ALU.mult).then_inc(ys_ready, 1)
            link(nc.vector.bn_stats(stats[:], ln_rows[:, 0]))
            link(nc.vector.bn_aggr(moments[:], stats[:]))
            link(nc.vector.tensor_scalar(ln_s[:, 0:1], moments[:, 1:2], LN_EPS, None, ALU.add))
            dve.wait_ge(dsum_ready, 1)
            nc.vector.tensor_scalar(var_d, ps_z[:, 0:P].rearrange("p (k b) -> p k b", b=B), L0_EPS, None, ALU.add)\
              .then_inc(var_ready, 2)
            dve.wait_ge(root_ready, 2)
            link(nc.vector.reciprocal(root_d, root_d))
            link(nc.vector.tensor_tensor(newton_d, root_d, root_d, ALU.mult))
            link(nc.vector.tensor_tensor(newton_d, newton_d, var_d, ALU.mult))
            link(nc.vector.tensor_scalar(newton_d, newton_d, -0.5, 1.5, ALU.mult, ALU.add))
            nc.vector.tensor_tensor(dT[:], newton_d, root_d, ALU.mult).then_inc(d_ready, 1)
            link(nc.vector.reciprocal(ln_s[:, 1:2], ln_s[:, 1:2]))
            link(nc.vector.tensor_tensor(ln_s[:, 2:3], ln_s[:, 1:2], ln_s[:, 1:2], ALU.mult))
            link(nc.vector.tensor_tensor(ln_s[:, 2:3], ln_s[:, 2:3], ln_s[:, 0:1], ALU.mult))
            link(nc.vector.tensor_scalar(ln_s[:, 2:3], ln_s[:, 2:3], -0.5, 1.5, ALU.mult, ALU.add))
            link(nc.vector.tensor_tensor(ln_s[:, 3:4], ln_s[:, 2:3], ln_s[:, 1:2], ALU.mult))
            link(nc.vector.tensor_scalar(ae, ln_rows[:, 0], moments[:, 0:1], ln_s[:, 3:4], ALU.subtract, ALU.mult))
            link(nc.vector.tensor_tensor(ae, ae, ln_rows[:, 1], ALU.mult))
            nc.vector.tensor_tensor(ae, ae, ln_rows[:, 2], ALU.add).then_inc(ae_ready, 1)
            dve.wait_ge(aeT_ps, 1)
            nc.vector.tensor_copy(aeT[:], ps_z[:, 0:P].rearrange("p (k b) -> p k b", b=B)).then_inc(aeT_ready, 1)
            dve.wait_ge(u_ps, 1)
            nc.vector.tensor_tensor(ae, ps_x3[0:B, :], ln_rows[:, 3], ALU.add).then_inc(u_ready, 1)
            dve.wait_ge(hyperT_ps, 1)
            nc.vector.tensor_copy(hyperT[:], ps_z[:, 0:P].rearrange("p (k b) -> p k b", b=B)).then_inc(hyperT_ready, 1)

            link(nc.vector.memset(absmax[:], 1.0))
            link(nc.vector.tensor_reduce(absmax[:, 0:1], condT_sb[:].rearrange("p k b -> p (k b)"), AX.X, ALU.max,
                                         apply_absolute_value=True))
            nc.vector.tensor_scalar(absmax[:, 0:1], absmax[:, 0:1], 1.0, None, ALU.max)
            dve.wait_ge(ld_wh1, 16)
            nc.vector.tensor_reduce(absmax[:, 1:2], wh1_staged[:].rearrange("p k n -> p (k n)"), AX.X, ALU.max,
                                    apply_absolute_value=True)
            for k in range(KC):
                slot, landed = staged(STAGED_WH3 + k)
                dve.wait_ge(ld_ring[slot], landed)
            nc.vector.tensor_reduce(absmax[:, 2:3], shared[:].rearrange("p r n -> p (r n)"), AX.X, ALU.max,
                                    apply_absolute_value=True).then_inc(absmax_ready, 1)
            dve.wait_ge(absmax_ps, 1)
            link(nc.vector.tensor_reduce(absmax_all[:], ps_z[0:4, 0:P], AX.X, ALU.max))
            nc.vector.tensor_scalar(absmax_diag[:], ident[0:4, 0:4], absmax_all[:], None, ALU.mult).then_inc(diag_ready, 1)
            dve.wait_ge(spread_ps, 1)
            link(nc.vector.tensor_scalar(absmax[:], ps_z[:, 0:4], 2.0 ** -60, None, ALU.max))
            link(nc.vector.tensor_scalar(absmax[:].bitcast(i32), absmax[:].bitcast(i32), 0x7F800000, None,
                                         ALU.bitwise_and))
            nc.vector.tensor_scalar(scales[:].bitcast(i32), absmax[:].bitcast(i32), -1.0, float(267 << 23),
                                    ALU.mult, ALU.add).then_inc(scales_ready, 1)
            dve.wait_ge(scales_ready, 1)
            link(nc.vector.tensor_scalar(unscales[:], scales[:], s_h, None, ALU.mult))
            nc.vector.tensor_scalar(unscales[:].bitcast(i32), unscales[:].bitcast(i32), -1.0, float(254 << 23),
                                    ALU.mult, ALU.add).then_inc(scales_ready, 1)
            dve.wait_ge(hi_ready, 2)
            nc.vector.scalar_tensor_tensor(rnn_h16[:, :, 1], condT_sb[:], s_h, rnn_h16[:, :, 0],
                                           ALU.mult, ALU.subtract).then_inc(split_ready, 1)
            nc.vector.scalar_tensor_tensor(lstm_h16[:, 1], condT_sb[:], s_h, lstm_h16[:, 0],
                                           ALU.mult, ALU.subtract).then_inc(split_ready, 1)
            dve.wait_ge(hi_ready, 3)
            nc.vector.scalar_tensor_tensor(wh1_lo[:], wh1_staged[:], s_wh1, wh1_hi[:],
                                           ALU.mult, ALU.subtract).then_inc(split_ready, 1)
            for k in range(KC):
                slot, _ = staged(STAGED_WH3 + k)
                dve.wait_ge(hi_ready, 3 + k + 1)
                nc.vector.scalar_tensor_tensor(wh3_lo[:, k], shared[:, slot], s_wh3, wh3_hi[:, k],
                                               ALU.mult, ALU.subtract).then_inc(split_ready, 1)

            dve.wait_ge(ld_b2, 16 * 4 * RH)
            for q in range(4):
                dve.wait_ge(w2_used, RH * (q + 1))
                dst = a_rows if q < 2 else b_all
                nc.vector.tensor_tensor(dst[:, q % 2], ps_xw[q % 2][:], b2_bc[:, q], ALU.add).then_inc(rows_ready, 1)
            for half in range(2):
                dve.wait_ge(a_ps, half + 1)
                src = ps_lstm_t if half == 0 else ps_rnn
                nc.vector.tensor_copy(a_all[:, :, half], src[:].rearrange("p (k n) -> p k n", k=KC)).then_inc(a_ready, 1)
            dve.wait_ge(ld_rnn, 32)
            dve.wait_ge(ld_b3, 16)
            dve.wait_ge(consts_ready, 3 + RH)
            dve.wait_ge(wx3_ready, KC)

            def iteration(m, p, has, i):
                q1 = (p + 1) % 2

                def xw_evac(j):
                    a = tile_no(m, p, 1)
                    wait(dve, xw_ps, step_no(m, p, 1, j + 1))
                    wait(dve, xw_moved[p], MOVES * (turn(m, p, 2) + 1))
                    nc.vector.tensor_tensor(xw_tok[:, j], ps_xw[j % 2][:], b3_bc[:, GW * j:GW * j + GW], ALU.add)\
                      .then_inc(xw_ready, 1)

                for s in range(STEPS):
                    t, r = step_no(m, p, 2, s), step_no(m, p, 0, s)
                    if has[3]:
                        wait(dve, gates_ps, t + 1)
                        if s == 0:
                            wait(dve, xw_moved[p], MOVES * (turn(m, p, 2) + 1))
                        nc.vector.scalar_tensor_tensor(gates[:], ps_gates[:], un_lstm, xw_step[p][:, s],
                                                       ALU.mult, ALU.add).then_inc(gates_ready, 1)
                    if has[1]:
                        wait(dve, rnn_ps, r + 1)
                        if s == 0:
                            wait(dve, xw1_ready, tile_no(m, p, 0) + 1)
                        sums = ps_rnn[:, 0:2 * P].rearrange("p (k h b) -> p k h b", h=2, b=B)
                        nc.vector.scalar_tensor_tensor(rnn_half[:], sums[:, :, 1], un_rnn, xw1T[:, :, s],
                                                       ALU.mult, ALU.add).then_inc(rnn_half_ready, 1)
                        wait(dve, rnn_half_ready, r + 1)
                        nc.vector.scalar_tensor_tensor(rnn_pre[:], sums[:, :, 0], un_rnn, rnn_half[:],
                                                       ALU.mult, ALU.add).then_inc(rnn_pre_ready, 1)
                    if has[3]:
                        wait(dve, gates_acted, 2 * t + 2)
                        nc.vector.tensor_tensor(kept[:], gate_act[:, P:2 * P], cell[:], ALU.mult)
                        nc.vector.tensor_tensor(added[:], gate_act[:, 0:P], gate_act[:, 3 * P:GW], ALU.mult)\
                          .then_inc(added_ready, 1)
                        wait(dve, added_ready, t + 1)
                        nc.vector.tensor_tensor(cell[:], kept[:], added[:], ALU.add).then_inc(cell_ready, 1)
                    if has[1]:
                        wait(dve, rnn_hi_ready, r + 1)
                        nc.vector.scalar_tensor_tensor(rnn_h16[:, :, 1], rnn_h[:], s_h, rnn_h16[:, :, 0],
                                                       ALU.mult, ALU.subtract).then_inc(rnn_lo_ready, 1)
                        nc.vector.tensor_tensor(x2T[p][:, :, s], x1T[p][:, :, s], rnn_h[:], ALU.add).then_inc(x2_ready, 1)
                    if has[3]:
                        wait(dve, cell_tanh_ready, t + 1)
                        nc.vector.tensor_tensor(lstm_h[:], gate_act[:, 2 * P:3 * P], cell_tanh[:], ALU.mult)\
                          .then_inc(lstm_h_ready, 1)
                        wait(dve, lstm_hi_ready, t + 1)
                        hT = ps_lstm_t[:, 0:P].rearrange("p (k b) -> p k b", b=B)
                        nc.vector.scalar_tensor_tensor(lstm_h16[:, 1], hT, s_h, lstm_h16[:, 0],
                                                       ALU.mult, ALU.subtract).then_inc(lstm_lo_ready, 1)
                        nc.vector.tensor_tensor(x3T[p][:, :, s], hT, x3T[p][:, :, s], ALU.add).then_inc(out_ready, 1)
                    if has[0] and s == 0:
                        a = tile_no(m, p, -1)
                        wait(dve, l0_ready, a + 1)
                        nc.vector.tensor_tensor(x1T[q1], ps_feat[:].rearrange("p (k t b) -> p k t b", t=STEPS, b=B),
                                                dT[:].unsqueeze(2).broadcast_to([P, KC, STEPS, B]), ALU.mult)\
                          .then_inc(l0_scaled, 1)
                        wait(dve, l0_scaled, a + 1)
                        nc.vector.tensor_tensor(x1T[q1], x1T[q1], xT_sb[q1][:], ALU.add).then_inc(x1_ready, 1)
                    if has[2] and s == 0:
                        a = tile_no(m, p, 1)
                        wait(dve, z_ready, a + 1)
                        nc.vector.tensor_tensor(zm[:].rearrange("p h t b -> p (h t) b"),
                                                ps_z[:, 0:2 * P].rearrange("p (n b) -> p n b", b=B),
                                                same_b[:].unsqueeze(1).broadcast_to([P, 2 * STEPS, B]), ALU.mult)\
                          .then_inc(zm_ready, 1)
                    if has[2] and s == 1:
                        a = tile_no(m, p, 1)
                        wait(dve, x3_ps, a + 1)
                        wait(dve, st_out[q1], 16 * turn(m, p, 1))
                        nc.vector.scalar_tensor_tensor(x3T[q1].rearrange("p k t b -> p (k t b)"),
                                                       x2T[q1].rearrange("p k t b -> p (k t b)"), 2.0, ps_x3[:],
                                                       ALU.mult, ALU.add).then_inc(x3_ready, 1)
                    if has[2] and s >= 2:
                        xw_evac(2 * (s - 2))
                        xw_evac(2 * (s - 2) + 1)
                    if has[0] and s == 3:
                        a = tile_no(m, p, -1)
                        wait(dve, xw1_ps, a + 1)
                        nc.vector.tensor_tensor(xw1T.rearrange("p k t b -> p k (t b)"),
                                                ps_feat[:].rearrange("p (k n) -> p k n", k=KC),
                                                b1T_sb[:].unsqueeze(2).broadcast_to([P, KC, TOK]), ALU.add)\
                          .then_inc(xw1_ready, 1)

            pipeline(dve, iteration)

        @block.tensor
        def _(pe):
            pe.wait_ge(ys_ready, 2)
            for oc in range(KC):
                for k in range(KC):
                    last = nc.tensor.matmul(ps_z[:, B * oc:B * oc + B], w0_sq[:, k, P * oc:P * oc + P], ysq[:, k],
                                            start=(k == 0), stop=(k == KC - 1))
            last.then_inc(dsum_ready, 1)
            pe.wait_ge(consts_ready, 3 + RH)
            pe.wait_ge(ae_ready, 1)
            for k in range(KC):
                last = nc.tensor.transpose(ps_z[:, B * k:B * k + B], ae[:, P * k:P * k + P], ident[0:B, 0:B])
            last.then_inc(aeT_ps, 1)
            pe.wait_ge(ld_w1, 16)
            pe.wait_ge(aeT_ready, 1)
            for k in range(KC):
                last = nc.tensor.matmul(ps_x3[0:B, :], aeT[:, k], w1_sb[:, k], start=(k == 0), stop=(k == KC - 1))
            last.then_inc(u_ps, 1)
            pe.wait_ge(hyper_ready, 1)
            for k in range(KC):
                last = nc.tensor.transpose(ps_z[:, B * k:B * k + B], hyper[:, P * k:P * k + P], ident[0:B, 0:B])
            last.then_inc(hyperT_ps, 1)
            pe.wait_ge(hyperT_ready, 1)
            pe.wait_ge(absmax_ready, 1)
            nc.tensor.transpose(ps_z[0:4, 0:P], absmax[:], ident[:]).then_inc(absmax_ps, 1)
            pe.wait_ge(diag_ready, 1)
            nc.tensor.matmul(ps_z[:, 0:4], ones[:], absmax_diag[:], start=True, stop=True).then_inc(spread_ps, 1)
            for n in range(2 * RANK):
                q, j = n // RH, n % RH
                if q >= 2 and j == 0:
                    pe.wait_ge(rows_ready, q - 1)
                slot, landed = staged(STAGED_W2 + n)
                pe.wait_ge(ld_ring[slot], landed)
                for k in range(KC):
                    last = nc.tensor.matmul(ps_xw[q % 2][B * j:B * j + B, :], hyperT[:, k], ring[:, slot, k],
                                            start=(k == 0), stop=(k == KC - 1), tile_position=(0, B * j))
                last.then_inc(w2_used, 1)
            for half in range(2):
                pe.wait_ge(rows_ready, half + 1)
                dst = ps_lstm_t if half == 0 else ps_rnn
                for k in range(KC):
                    last = nc.tensor.transpose(dst[:, P * k:P * k + P], a_rows[:, half, P * k:P * k + P], ident[:])
                last.then_inc(a_ps, 1)
            pe.wait_ge(rows_ready, 4)
            pe.wait_ge(a_ready, 2)
            pe.wait_ge(split_ready, 3 + KC)
            pe.wait_ge(wx3_ready, KC)
            pe.wait_ge(ld_rnn, 32)
            pe.wait_ge(ld_base, 16)

            def l0(chunks):
                for oc in chunks:
                    for k in range(KC):
                        last = nc.tensor.matmul(ps_feat[:, TOK * oc:TOK * oc + TOK], w0_sb[:, k, P * oc:P * oc + P],
                                                xs[:, k], start=(k == 0), stop=(k == KC - 1))
                return last

            def xw1(q, chunks):
                for oc in chunks:
                    for k in range(KC):
                        last = nc.tensor.matmul(ps_feat[:, TOK * oc:TOK * oc + TOK], wx1_sb[:, k, P * oc:P * oc + P],
                                                x1T[q][:, k], start=(k == 0), stop=(k == KC - 1))
                return last

            def x3(q, chunks):
                for oc in chunks:
                    for k in range(KC):
                        nc.tensor.matmul(ps_x3[:, TOK * oc:TOK * oc + TOK], base_sb[:, k, P * oc:P * oc + P],
                                         x2T[q][:, k], start=(k == 0), stop=False)
                    for half in range(2):
                        last = nc.tensor.matmul(ps_x3[:, TOK * oc:TOK * oc + TOK], b_all[:, half, P * oc:P * oc + P],
                                                zm[:, half], start=False, stop=(half == 1))
                return last

            def xw(j):
                parts = [(x3_hi, wx3_hi), (x3_hi, wx3_lo), (x3_lo, wx3_hi)]
                for n, (x, w) in enumerate(parts):
                    for k in range(KC):
                        last = nc.tensor.matmul(ps_xw[j % 2][:], x[:, k], w[:, k, GW * j:GW * j + GW],
                                                start=(n == 0 and k == 0), stop=(n == 2 and k == KC - 1))
                return last

            def lstm_product():
                parts = [(0, wh3_hi), (0, wh3_lo), (1, wh3_hi)]
                for n, (part, w) in enumerate(parts):
                    for k in range(KC):
                        for j in range(KC):
                            last = nc.tensor.matmul(ps_gates[B * j:B * j + B, :], lstm_h16[:, part, k],
                                                    w[:, k, GW * j:GW * j + GW], start=(n == 0 and k == 0),
                                                    stop=(n == 2 and k == KC - 1), tile_position=(0, B * j))
                return last

            def rnn_product():
                for oc in range(KC):
                    at = 2 * B * oc
                    for k in range(KC):
                        nc.tensor.matmul(ps_rnn[:, at:at + 2 * B], wh1_hi[:, k, P * oc:P * oc + P],
                                         rnn_h16[:, k].rearrange("p h b -> p (h b)"), start=(k == 0), stop=False)
                    for k in range(KC):
                        last = nc.tensor.matmul(ps_rnn[:, at:at + B], wh1_lo[:, k, P * oc:P * oc + P], rnn_h16[:, k, 0],
                                                start=False, stop=(k == KC - 1))
                return last

            def iteration(m, p, has, i):
                q1 = (p + 1) % 2
                for s in range(STEPS):
                    t, r = step_no(m, p, 2, s), step_no(m, p, 0, s)
                    if has[3]:
                        wait(pe, lstm_lo_ready, t)
                        lstm_product().then_inc(gates_ps, 1)
                    if has[1]:
                        wait(pe, rnn_lo_ready, r)
                        rnn_product().then_inc(rnn_ps, 1)
                    if s == 0 and has[0]:
                        wait(pe, xs_ready, tile_no(m, p, -1) + 1)
                        wait(pe, xw1_ready, tile_no(m, p, 0) + 1 if has[1] else 0)
                        l0(range(KC)).then_inc(l0_ready, 1)
                    if s == 1 and has[2]:
                        wait(pe, zm_ready, tile_no(m, p, 1) + 1)
                        x3(q1, (0, 1))
                    if s == 2 and has[2]:
                        wait(pe, x3_lo_ready, tile_no(m, p, 1) + 1)
                    if s >= 2 and has[2]:
                        wait(pe, xw_ready, step_no(m, p, 1, 0) + 2 * (s - 2) - 1)
                        xw(2 * (s - 2)).then_inc(xw_ps, 1)
                    if has[3]:
                        wait(pe, lstm_h_ready, t + 1)
                        nc.tensor.transpose(ps_lstm_t[:, 0:P], lstm_h[:], ident[:]).then_inc(lstm_t_ps, 1)
                    if s == 0 and has[2]:
                        wait(pe, x2_ready, step_no(m, p, 1, STEPS))
                        for half in range(2):
                            for k in range(KC):
                                last = nc.tensor.matmul(ps_z[:, P * half:P * half + P], a_all[:, k, half], x2T[q1][:, k],
                                                        start=(k == 0), stop=(k == KC - 1))
                        last.then_inc(z_ready, 1)
                    if s == 1 and has[2]:
                        x3(q1, (2, 3)).then_inc(x3_ps, 1)
                    if s >= 2 and has[2]:
                        wait(pe, xw_ready, step_no(m, p, 1, 0) + 2 * (s - 2))
                        xw(2 * (s - 2) + 1).then_inc(xw_ps, 1)
                    if s == 2 and has[0]:
                        wait(pe, x1_ready, tile_no(m, p, -1) + 1)
                        xw1(q1, (0, 1))
                    if s == 3 and has[0]:
                        xw1(q1, (2, 3)).then_inc(xw1_ps, 1)

            pipeline(pe, iteration)


def kernel(**inputs):
    import numpy as np
    import concourse.bacc as bacc
    from concourse.bass_utils import run_bass_kernel_spmd

    a = {k: np.asarray(v) for k, v in inputs.items()}
    feature_major = (TILES, STEPS, B, KC, P)

    def gates_by_chunk(w):
        return w.reshape(-1, GATES, KC, P).transpose(0, 2, 1, 3).reshape(w.shape[0] if w.ndim > 1 else KC, -1)

    arrays = {
        "xT": a["x"].transpose(1, 0, 2).reshape(feature_major).transpose(0, 4, 3, 1, 2),
        "condT": a["cond_1024"].reshape(B, KC, P).transpose(2, 1, 0),
        "cond": a["cond_1024"],
        "w0": a["L0_cond_weight"],
        "wx1": a["L1_cond_Wx"], "wh1": a["L1_cond_Wh"], "b1T": a["L1_cond_b"].reshape(KC, P).T,
        "base": a["L2_cond_base_layer"],
        "hw1": a["L2_cond_w1"], "hb1": a["L2_cond_b1"],
        "hw2": a["L2_cond_w2"].reshape(-1, 2, D, RANK).transpose(1, 3, 0, 2),
        "hb2": a["L2_cond_b2"].reshape(2, D, RANK).transpose(0, 2, 1),
        "ln_g": a["L2_cond_ln_g"], "ln_b": a["L2_cond_ln_b"],
        "wx3": gates_by_chunk(a["L3_cond_Wx"]), "wh3": gates_by_chunk(a["L3_cond_Wh"]),
        "b3": gates_by_chunk(a["L3_cond_b"]),
    }
    nc = bacc.Bacc("TRN2", target_bir_lowering=False, num_devices=1)
    fed, args = {}, []
    for name, v in arrays.items():
        v = np.ascontiguousarray(v)
        fed[f"in_{name}"] = v
        args.append(nc.dram_tensor(f"in_{name}", v.shape, mybir.dt.from_np(v.dtype), kind="ExternalInput").ap())
    out = nc.dram_tensor("outT", (TILES, P, KC, STEPS, B), mybir.dt.float32, kind="ExternalOutput").ap()
    build(nc, *args, out)
    r = run_bass_kernel_spmd(nc, [fed], core_ids=[0])
    got = r.results[0]["outT"]
    return got.transpose(4, 0, 3, 2, 1).reshape(B, T, D)
```

```python
import concourse.bass as bass
from concourse import mybir
from contextlib import ExitStack

B, T, D, H, RANK = 32, 128, 512, 512, 8
P = 128
KC = D // P
STEPS = 4
TOK = STEPS * B
TILES = T // STEPS
GATES = 4
GW = GATES * P
RH = RANK // 2
BH = B // 2
ZN = STEPS * BH
RING = 4
TOP = 13
LEAST = 2.0 ** -30
X1_SHIFT = 5
X2_SHIFT = 6
Z_SHIFT = 23
FIRST_MOVES = 16 * KC
MOVES = 16 * (STEPS - 1) * KC
LN_EPS = 1e-5
L0_EPS = 1e-8


def build(nc, xT, condT, cond, w0, wx1, wh1, b1T, base, hw1, hb1T, hw2, hb2, ln_g, ln_b, wx3, wh3, b3, out):
    fp32 = mybir.dt.float32
    f32r = mybir.dt.float32r
    fp16 = mybir.dt.float16
    i32 = mybir.dt.int32
    ALU = mybir.AluOpType
    ACT = mybir.ActivationFunctionType
    AX = mybir.AxisListType

    ctx = ExitStack()
    with ctx:
        def sb(name, shape, dt=fp32):
            return ctx.enter_context(nc.sbuf_tensor(name, shape, dt))

        def sem(name):
            return ctx.enter_context(nc.semaphore(name))

        def bank(name):
            return ctx.enter_context(nc.psum_tensor(name, [P, 512], fp32))

        def over(name, shape, dt, offset):
            return nc.alloc_sbuf_tensor_at(name, shape, dt, offset=offset)

        w0_hi, w0_lo = sb("w0_hi", [P, KC, D], fp16), sb("w0_lo", [P, KC, D], fp16)
        wx1_hi, wx1_lo = sb("wx1_hi", [P, KC, H], fp16), sb("wx1_lo", [P, KC, H], fp16)
        wh1_hi, wh1_lo = sb("wh1_hi", [P, KC, H], fp16), sb("wh1_lo", [P, KC, H], fp16)
        base_hi, base_lo = sb("base_hi", [P, KC, D], fp16), sb("base_lo", [P, KC, D], fp16)
        a_hi, a_lo = sb("a_hi", [P, 2, KC, P], fp16), sb("a_lo", [P, 2, KC, P], fp16)
        b_hi, b_lo = sb("b_hi", [P, 2, D], fp16), sb("b_lo", [P, 2, D], fp16)
        w0_sq = over("w0_sq", [P, KC, D], fp32, nc.sbuf_base)
        wh3_hi = sb("wh3_hi", [P, KC, KC * GW], fp16)
        wh3_lo = sb("wh3_lo", [P, KC, KC * GW], fp16)
        wh3_staged = over("wh3_staged", [P, KC, KC * GW], fp32, nc.sbuf_base)
        wx3_hi = sb("wx3_hi", [P, KC, KC * GW], f32r)
        ring = over("ring", [P, RING, KC, D], fp32, nc.sbuf_base)
        wx3_lo = sb("wx3_lo", [P, KC, KC * GW], f32r)
        b1T_sb = sb("b1T_sb", [P, KC])
        hb1T_sb = sb("hb1T_sb", [P, KC])
        b3_bc = sb("b3_bc", [P, KC * GW])
        b2_bc = b3_bc[:].rearrange("p (q n) -> p q n", q=4)
        w1_sb = b3_bc[:].rearrange("p (k n) -> p k n", k=KC)
        ident = sb("ident", [P, P])
        same_b = sb("same_b", [P, BH])
        condT_sb = sb("condT_sb", [P, KC, B])
        ysT = sb("ysT", [P, KC, B])
        dT = sb("dT", [P, KC, B])
        rows_at = nc.sbuf_base
        rows = sb("rows", [P, 4, D])
        ln_rows = rows[0:B]
        ae = ln_rows[:, 0]
        b_rows, a_rows = rows[:, 0:2], rows[:, 2:4]
        stats, moments, ln_s = ln_rows[:, 3, 0:6], ln_rows[:, 3, 8:10], ln_rows[:, 3, 12:16]

        absmax = sb("absmax", [P, 11])
        absmax_all = sb("absmax_all", [P, 11])
        exps = sb("exps", [P, 9])
        scales = sb("scales", [P, 9])
        s_w0, s_wx1, s_wh1, s_a, s_wh3, s_h = (scales[:, n:n + 1] for n in (1, 2, 3, 5, 7, 8))
        unscales = sb("unscales", [P, 2])
        un_rnn, un_lstm = unscales[:, 0:1], unscales[:, 1:2]
        l2_scales = sb("l2_scales", [P, 4])
        s_base, s_b = l2_scales[:, 0:1], l2_scales[:, 1:2]
        m_part = sb("m_part", [P, 1])
        m_all = sb("m_all", [P, 1])
        m_least = sb("m_least", [P, 3])
        m_exp = sb("m_exp", [P, 3])
        m_scale = sb("m_scale", [P, 3])
        m_shift = sb("m_shift", [P, 3])
        tile_w = sb("tile_w", [P, 2])
        tile_p = sb("tile_p", [P, 2])
        tile_s = [sb(f"tile_s{q}", [P, 5]) for q in range(2)]
        d_un = sb("d_un", [P, KC, B])
        x2_s = sb("x2_s", [P, 2])

        shared = sb("shared", [P, 3, KC * D])
        xw_step = [shared[:, q].rearrange("p (t n) -> p t n", t=STEPS) for q in range(2)]
        xw_tok = shared[:, 2].rearrange("p (j n) -> p j n", j=KC)
        W0_SLOT, WH1_SLOT, WX1_SLOT = 0, 1, 2
        b_halves = shared[:, 2, 0:2 * D].rearrange("p (h n) -> p h n", h=2)
        WX3_SLOT = [0, 1, 0, 1]
        late = sb("late", [P, KC * D])
        x3T = [late[:, TOK * KC * q:TOK * KC * (q + 1)].rearrange("p (k t b) -> p k t b", k=KC, t=STEPS) for q in range(2)]
        kept = late[:, 1024:1024 + P]
        zm = late[:, 1536:1536 + TOK].rearrange("p (h t b) -> p h t b", h=2, t=STEPS)
        zm16 = late[:, 1792:1792 + TOK].bitcast(fp16).rearrange("p (a h n) -> p a h n", a=2, h=2)
        xT_sb = [sb(f"xT_sb{q}", [P, KC, STEPS, B]) for q in range(2)]
        x1T = [sb(f"x1T{q}", [P, KC, STEPS, B]) for q in range(2)]
        x2T = [sb("x2T0", [P, KC, STEPS, B]), over("x2T1", [P, KC, STEPS, B], fp32, rows_at)]
        xw1T = sb("xw1T", [P, KC, STEPS, B])
        xs16 = sb("xs16", [P, 2, KC, TOK], fp16)
        x1_16 = sb("x1_16", [P, 2, KC, TOK], fp16)
        x2_16 = over("x2_16", [P, 2, KC, TOK], fp16, rows_at + 4 * D)
        x3_hi = over("x3_hi", [P, KC, TOK], f32r, rows_at + 8 * D)
        x3_lo = over("x3_lo", [P, KC, TOK], f32r, rows_at + 12 * D)
        rnn_half = sb("rnn_half", [P, KC, B])
        rnn_pre = sb("rnn_pre", [P, KC, B])
        rnn_h = sb("rnn_h", [P, KC, B])
        rnn_h16 = sb("rnn_h16", [P, KC, 2, B], fp16)
        cell = sb("cell", [P, P])
        added = sb("added", [P, P])
        cell_tanh = sb("cell_tanh", [P, P])
        lstm_h = sb("lstm_h", [P, P])
        lstm_h16 = sb("lstm_h16", [P, 2, KC, B], fp16)
        ysq, aeT, hyperT = (x[:].rearrange("p (k b) -> p k b", b=B) for x in (added, cell_tanh, lstm_h))
        var_d, root_d, newton_d = rnn_half[:], rnn_pre[:], rnn_h[:]

        ps_feat = bank("ps_feat")
        ps_rnn = bank("ps_rnn")
        ps_z = bank("ps_z")
        ps_x3 = bank("ps_x3")
        ps_xw = [bank("ps_xw0"), bank("ps_xw1")]
        ps_gates = bank("ps_gates")
        ps_lstm_t = bank("ps_lstm_t")
        ps_turned = [ps_x3, ps_z]
        ps_rows = [ps_xw[0], ps_xw[1], ps_gates, ps_lstm_t]

        ld_cond = sem("ld_cond")
        ld_w0 = sem("ld_w0")
        ld_wh1 = sem("ld_wh1")
        ld_wx1 = sem("ld_wx1")
        ld_w1 = sem("ld_w1")
        ld_wh3 = [sem(f"ld_wh3_{k}") for k in range(KC)]
        ld_base = sem("ld_base")
        ld_b1 = sem("ld_b1")
        ld_b2 = sem("ld_b2")
        ld_b3 = sem("ld_b3")
        ld_ring = [sem(f"ld_ring{n}") for n in range(RING)]
        ld_wx3 = [sem(f"ld_wx3_{k}") for k in range(KC)]
        ld_x = [sem("ld_x0"), sem("ld_x1")]
        xw_moved_first = [sem("xw_moved_first0"), sem("xw_moved_first1")]
        xw_moved = [sem("xw_moved0"), sem("xw_moved1")]
        st_out = [sem("st_out0"), sem("st_out1")]
        consts_cleared = sem("consts_cleared")
        consts_ready = sem("consts_ready")
        ys_ready = sem("ys_ready")
        dve_set = sem("dve_set")
        dsum_ready = sem("dsum_ready")
        ln_var_ready = sem("ln_var_ready")
        ln_root_ready = sem("ln_root_ready")
        d_var_ready = sem("d_var_ready")
        d_root_ready = sem("d_root_ready")
        ae_ready = sem("ae_ready")
        aeT_ps = sem("aeT_ps")
        aeT_ready = sem("aeT_ready")
        u_ps = sem("u_ps")
        u_ready = sem("u_ready")
        hyper_ready = sem("hyper_ready")
        absmax_ready = sem("absmax_ready")
        absmax_spread = sem("absmax_spread")
        scales_ready = sem("scales_ready")
        h0_hi, h0_lo = sem("h0_hi"), sem("h0_lo")
        w_hi_ready = sem("w_hi_ready")
        w_lo_ready = sem("w_lo_ready")
        wh3_hi_ready, wh3_lo_ready = sem("wh3_hi_ready"), sem("wh3_lo_ready")
        l2_hi_ready, l2_lo_ready = sem("l2_hi_ready"), sem("l2_lo_ready")
        wx3_hi_ready = sem("wx3_hi_ready")
        wx3_lo_ready = [sem(f"wx3_lo_ready{k}") for k in range(KC)]
        w2_used = sem("w2_used")
        b_moved = sem("b_moved")
        rows_ready = sem("rows_ready")
        a_ps = sem("a_ps")
        m_ready = sem("m_ready")
        m_spread = sem("m_spread")
        tile_s_chain = sem("tile_s_chain")
        tile_s_ready = sem("tile_s_ready")
        x2_s_chain = sem("x2_s_chain")
        x2_s_ready = sem("x2_s_ready")
        xs_ready = sem("xs_ready")
        xs_hi_ready, xs_lo_ready = sem("xs_hi_ready"), sem("xs_lo_ready")
        x1_hi_ready, x1_lo_ready = sem("x1_hi_ready"), sem("x1_lo_ready")
        x2_hi_ready, x2_lo_ready = sem("x2_hi_ready"), sem("x2_lo_ready")
        zm_hi_ready, zm_lo_ready = sem("zm_hi_ready"), sem("zm_lo_ready")
        x3_scaled = sem("x3_scaled")
        l0_ready = sem("l0_ready")
        l0_scaled = sem("l0_scaled")
        x1_ready = sem("x1_ready")
        xw1_ps = sem("xw1_ps")
        xw1_ready = sem("xw1_ready")
        z_ready = sem("z_ready")
        zm_ready = sem("zm_ready")
        x3_ps = sem("x3_ps")
        x3_ready = sem("x3_ready")
        x3_hi_ready = sem("x3_hi_ready")
        x3_lo_ready = sem("x3_lo_ready")
        xw_ps = sem("xw_ps")
        xw_ready = sem("xw_ready")
        rnn_ps = sem("rnn_ps")
        rnn_half_ready = sem("rnn_half_ready")
        rnn_pre_ready = sem("rnn_pre_ready")
        rnn_h_ready = sem("rnn_h_ready")
        rnn_hi_ready = sem("rnn_hi_ready")
        rnn_lo_ready = sem("rnn_lo_ready")
        x2_ready = sem("x2_ready")
        gates_ps = sem("gates_ps")
        gates_ready = sem("gates_ready")
        gates_acted = sem("gates_acted")
        added_ready = sem("added_ready")
        cell_ready = sem("cell_ready")
        cell_tanh_ready = sem("cell_tanh_ready")
        lstm_h_ready = sem("lstm_h_ready")
        lstm_t_ps = sem("lstm_t_ps")
        lstm_hi_ready = sem("lstm_hi_ready")
        lstm_lo_ready = sem("lstm_lo_ready")
        out_ready = sem("out_ready")

        def a_turned(n, half):
            return ps_turned[n][:].rearrange("p (c b) -> p c b", b=B)[:, :, BH * half:BH * half + BH]

        def a_part(a, n, half):
            return a[:, half, 2 * n:2 * n + 2].rearrange("p k c -> p (k c)").rearrange("p (c b) -> p c b", b=BH)

        block = ctx.enter_context(nc.Block())

        TILE_S_LINKS = 5

        def stages(i):
            return [0 <= i + k < TILES for k in (1, 0, -1, -2, 2)]

        HEAD = [-1, 0, 1, 2, 3]
        TAIL = [30, 31, 32, 33]

        def pipeline(engine, iteration, prepare=None, second_setup=None):
            def ahead(i):
                if prepare and i <= TAIL[-1]:
                    prepare(i // 2, i % 2, stages(i), i)

            ahead(HEAD[0])
            for i in HEAD:
                iteration(i // 2, i % 2, stages(i), i)
                if i == 0 and second_setup:
                    second_setup()
                ahead(i + 1)
            with engine.Fori(2, 15) as m:
                for p in range(2):
                    iteration(m, p, [True] * 5, None)
                    if prepare:
                        prepare(m + p, (p + 1) % 2, [True] * 5, None)
            for i in TAIL:
                iteration(i // 2, i % 2, stages(i), i)
                ahead(i + 1)

        def tile_no(m, p, lag):
            return 2 * m + (p - lag)

        def step_no(m, p, lag, s):
            return 8 * m + (4 * (p - lag) + s)

        def turn(m, p, lag):
            return m + (p - lag) // 2

        def wait(engine, sem_, value):
            if not isinstance(value, int) or value > 0:
                engine.wait_ge(sem_, value)

        @block.sync
        def _(sp):
            by_chunk = "(k p) n -> p k n"
            sp.dma_start(condT_sb[:], condT).then_inc(ld_cond, 16)
            sp.dma_start(ln_rows[:, 0], cond).then_inc(ld_cond, 16)
            sp.dma_start(ln_rows[:, 1], ln_g.partition_broadcast(B)).then_inc(ld_cond, 16)
            sp.dma_start(ln_rows[:, 2], ln_b.partition_broadcast(B)).then_inc(ld_cond, 16)
            sp.dma_start(hb1T_sb[:], hb1T).then_inc(ld_cond, 16)

            def load_weight(w, slot, landed):
                sp.dma_start(shared[:, slot].rearrange("p (k n) -> p k n", k=KC), w.rearrange(by_chunk, p=P))\
                  .then_inc(landed, 16)

            load_weight(w0, W0_SLOT, ld_w0)
            sp.dma_start(w1_sb, hw1.rearrange(by_chunk, p=P)).then_inc(ld_w1, 16)
            sp.dma_start(xT_sb[0][:], xT[0]).then_inc(ld_x[0], 16)
            load_weight(wx1, WX1_SLOT, ld_wx1)
            load_weight(wh1, WH1_SLOT, ld_wh1)
            sp.dma_start(xT_sb[1][:], xT[1]).then_inc(ld_x[1], 16)
            sp.dma_start(b1T_sb[:], b1T).then_inc(ld_b1, 16)

            def load_w2(n):
                sp.dma_start(ring[:, n % RING], hw2[1 - n // RANK, n % RANK].rearrange(by_chunk, p=P))\
                  .then_inc(ld_ring[n % RING], 16)

            for n in range(RING):
                load_w2(n)
            sp.wait_ge(u_ps, 1)
            for q in range(4):
                for j in range(RH):
                    sp.dma_start(b2_bc[B * j:B * j + B, q], hb2[1 - q // 2, RH * (q % 2) + j].partition_broadcast(B))\
                      .then_inc(ld_b2, 16)
            for n in range(RING, 2 * RANK):
                if n == RANK:
                    for k in range(KC):
                        sp.dma_start(wh3_staged[:, k], wh3[P * k:P * k + P]).then_inc(ld_wh3[k], 16)
                    sp.dma_start(late[:].rearrange("p (k n) -> p k n", k=KC), base.rearrange(by_chunk, p=P)).then_inc(ld_base, 16)
                if n == RANK + RING:
                    sp.wait_ge(rows_ready, 2)
                    sp.wait_ge(w_lo_ready, 3)
                    for q in range(2):
                        for j in range(RH):
                            for h in range(2):
                                at = BH * (RH * q + j)
                                sp.dma_start(b_halves[at:at + BH, h], rows[B * j + BH * h:B * j + BH * h + BH, q])\
                                  .then_inc(b_moved, 16)
                sp.wait_ge(w2_used, n - RING + 1)
                load_w2(n)
            for k in range(KC):
                if k < 2:
                    sp.wait_ge(w_lo_ready, 3)
                else:
                    sp.wait_ge(wx3_lo_ready[k - 2], 1)
                sp.dma_start(shared[:, WX3_SLOT[k]], wx3[P * k:P * k + P]).then_inc(ld_wx3[k], 16)
            sp.wait_ge(rows_ready, 4)
            sp.dma_start(b3_bc[:], b3.partition_broadcast(P)).then_inc(ld_b3, 16)

            def iteration(m, p, has, i):
                q1 = (p + 1) % 2
                if has[2]:
                    for j in range(KC):
                        wait(sp, xw_ready, step_no(m, p, 1, j + 1))
                        for s in range(STEPS):
                            sp.dma_start(xw_step[q1][B * j:B * j + B, s], xw_tok[B * s:B * s + B, j])\
                              .then_inc(xw_moved_first[q1] if s == 0 else xw_moved[q1], 16)
                if has[3]:
                    wait(sp, out_ready, step_no(m, p, 2, STEPS))
                    sp.dma_start(out[tile_no(m, p, 2)], x3T[p]).then_inc(st_out[p], 16)

            pipeline(sp, iteration)
            for q in range(2):
                sp.wait_ge(st_out[q], 16 * TILES // 2)

        @block.gpsimd
        def _(pool):
            MAX = bass.bass_isa.ReduceOp.max

            def wx3_low(k):
                pool.wait_ge(ld_wx3[k], 16)
                pool.wait_ge(wx3_hi_ready, k + 1)
                pool.wait_ge(w2_used, 2 * RANK)
                nc.gpsimd.tensor_tensor(wx3_lo[:, k], shared[:, WX3_SLOT[k]], wx3_hi[:, k].bitcast(fp32), ALU.subtract)\
                  .then_inc(wx3_lo_ready[k], 1)

            nc.gpsimd.memset(ident[:], 0.0).then_inc(consts_cleared, 1)
            nc.gpsimd.memset(same_b[:], 0.0).then_inc(consts_cleared, 1)
            nc.gpsimd.memset(cell[:], 0.0).then_inc(consts_ready, 1)
            pool.wait_ge(consts_cleared, 2)
            nc.gpsimd.affine_select(out=ident[:], in_=ident[:], compare_op=ALU.not_equal, fill=1.0, base=0,
                                    pattern=[[-1, P]], channel_multiplier=1).then_inc(consts_ready, 1)
            for g in range(RANK):
                nc.gpsimd.affine_select(out=same_b[:], in_=same_b[:], compare_op=ALU.not_equal, fill=1.0,
                                        base=-BH * g, pattern=[[-1, BH]], channel_multiplier=1)\
                  .then_inc(consts_ready, 1)
                pool.wait_ge(consts_ready, 3 + g)

            def spread(n, columns):
                pool.wait_ge(absmax_ready, n + 1)
                nc.gpsimd.partition_all_reduce(absmax_all[:, columns], absmax[:, columns], P, MAX)\
                  .then_inc(absmax_spread, 1)

            def spread_x():
                nc.gpsimd.partition_all_reduce(m_all[:], m_part[:], P, MAX).then_inc(m_spread, 1)

            spread(0, slice(0, 4))
            pool.wait_ge(m_ready, 1)
            spread_x()

            def second_setup():
                spread(1, slice(7, 11))

            def prepare(m, p, has, i):
                q1 = (p + 1) % 2
                if has[0]:
                    a = tile_no(m, p, -1)
                    wait(pool, ld_x[q1], 16 * (turn(m, p, -1) + 1))
                    wait(pool, ys_ready, 1 if i == -1 else 0)
                    wait(pool, x2_ready, step_no(m, p, 0, 0))
                    nc.gpsimd.tensor_tensor(x1T[q1][:], xT_sb[q1][:], ysT[:].unsqueeze(2).broadcast_to([P, KC, STEPS, B]),
                                            ALU.mult).then_inc(xs_ready, 1)

            def iteration(m, p, has, i):
                q1 = (p + 1) % 2
                if i == 1:
                    spread(2, slice(4, 7))
                    wx3_low(1)
                    wx3_low(2)
                if has[4]:
                    wait(pool, m_ready, tile_no(m, p, -2) + 1)
                    wait(pool, tile_s_ready, tile_no(m, p, -2))
                if has[2]:
                    a = tile_no(m, p, 1)
                    wait(pool, x3_hi_ready, a + 1)
                    nc.gpsimd.tensor_tensor(x3_lo[:], x3T[q1].rearrange("p k t b -> p k (t b)"),
                                            x3_hi[:].bitcast(fp32), ALU.subtract).then_inc(x3_lo_ready, 1)
                if has[4]:
                    spread_x()

            pipeline(pool, iteration, prepare, second_setup)

        @block.scalar
        def _(act):
            def high(out_, in_, scale):
                return nc.scalar.activation(out_, in_, ACT.Copy, scale=scale)

            def wx3_high(k):
                act.wait_ge(ld_wx3[k], 16)
                nc.scalar.copy(wx3_hi[:, k], shared[:, WX3_SLOT[k]]).then_inc(wx3_hi_ready, 1)

            def weight_high(w_hi, slot, s_w):
                high(w_hi[:].rearrange("p k n -> p (k n)"), shared[:, slot], s_w).then_inc(w_hi_ready, 1)

            act.wait_ge(ln_var_ready, 1)
            nc.scalar.activation(ln_s[:, 1:2], ln_s[:, 0:1], ACT.Sqrt).then_inc(ln_root_ready, 1)
            act.wait_ge(u_ready, 1)
            nc.scalar.activation(hyperT, hyperT, ACT.Gelu).then_inc(hyper_ready, 1)
            act.wait_ge(d_var_ready, 1)
            nc.scalar.activation(root_d, var_d, ACT.Sqrt).then_inc(d_root_ready, 1)
            act.wait_ge(scales_ready, 1)
            weight_high(w0_hi, W0_SLOT, s_w0)
            high(rnn_h16[:, :, 0], condT_sb[:], s_h).then_inc(h0_hi, 1)
            high(lstm_h16[:, 0], condT_sb[:], s_h).then_inc(h0_hi, 1)

            def second_setup():
                act.wait_ge(scales_ready, 2)
                for k in range(KC):
                    high(wh3_hi[:, k], wh3_staged[:, k], s_wh3).then_inc(wh3_hi_ready, 1)

            def l2_weights():
                act.wait_ge(scales_ready, 3)
                for n in range(2):
                    act.wait_ge(a_ps, n + 1)
                    for half in range(2):
                        high(a_part(a_hi, n, half), a_turned(n, half), s_a).then_inc(l2_hi_ready, 1)
                act.wait_ge(b_moved, 16 * 2 * RANK)
                high(b_hi[:], b_halves, s_b).then_inc(l2_hi_ready, 1)
                high(base_hi[:].rearrange("p k n -> p (k n)"), late[:], s_base).then_inc(l2_hi_ready, 1)

            def prepare(m, p, has, i):
                q1 = (p + 1) % 2
                if has[2]:
                    wait(act, x2_s_ready, tile_no(m, p, 1) + 1)
                    wait(act, x2_ready, step_no(m, p, 1, STEPS))
                    high(x2_16[:, 0], x2T[q1][:].rearrange("p k t b -> p k (t b)"), x2_s[:, 0:1]).then_inc(x2_hi_ready, 1)
                if has[0]:
                    a = tile_no(m, p, -1)
                    wait(act, tile_s_ready, a + 1)
                    wait(act, xs_ready, a + 1)
                    high(xs16[:, 0], x1T[q1][:].rearrange("p k t b -> p k (t b)"), tile_s[q1][:, 0:1])\
                        .then_inc(xs_hi_ready, 1)

            def load_x(m, p):
                wait(act, x1_ready, tile_no(m, p, 0) + 1)
                act.dma_start(xT_sb[p][:], xT[tile_no(m, p, -2)]).then_inc(ld_x[p], 16)

            def iteration(m, p, has, i):
                q1 = (p + 1) % 2
                if has[4] and (i is None or i > 0):
                    load_x(m, p)
                if i == -1:
                    weight_high(wx1_hi, WX1_SLOT, s_wx1)
                    weight_high(wh1_hi, WH1_SLOT, s_wh1)
                for s in range(STEPS):
                    t, r = step_no(m, p, 2, s), step_no(m, p, 0, s)
                    gates = xw_step[p][:, s]
                    if has[3]:
                        wait(act, gates_ready, 2 * t + 1)
                        nc.scalar.activation(gates[:, 0:2 * P], gates[:, 0:2 * P], ACT.Sigmoid).then_inc(gates_acted, 1)
                        wait(act, gates_ready, 2 * t + 2)
                        nc.scalar.activation(gates[:, 3 * P:GW], gates[:, 3 * P:GW], ACT.Tanh).then_inc(gates_acted, 1)
                        nc.scalar.activation(gates[:, 2 * P:3 * P], gates[:, 2 * P:3 * P], ACT.Sigmoid).then_inc(gates_acted, 1)
                    if has[1]:
                        wait(act, rnn_pre_ready, r + 1)
                        wait(act, x2_ready, r)
                        nc.scalar.activation(rnn_h[:], rnn_pre[:], ACT.Tanh).then_inc(rnn_h_ready, 1)
                        wait(act, rnn_h_ready, r + 1)
                        high(rnn_h16[:, :, 0], rnn_h[:], s_h).then_inc(rnn_hi_ready, 1)
                    if has[3]:
                        wait(act, cell_ready, t + 1)
                        nc.scalar.activation(cell_tanh[:], cell[:], ACT.Tanh).then_inc(cell_tanh_ready, 1)
                        wait(act, lstm_t_ps, t + 1)
                        high(lstm_h16[:, 0], ps_lstm_t[:, 0:P].rearrange("p (k b) -> p k b", b=B), s_h)\
                            .then_inc(lstm_hi_ready, 1)
                    if i == 1 and s == 0:
                        act.wait_ge(wh3_lo_ready, KC)
                        wx3_high(0)
                        wx3_high(1)
                        l2_weights()
                    if has[2] and s == 0:
                        wait(act, zm_ready, tile_no(m, p, 1) + 1)
                        high(zm16[:, 0], zm.rearrange("p h t b -> p h (t b)"), 2.0 ** -Z_SHIFT).then_inc(zm_hi_ready, 1)
                    if has[0] and s == 0:
                        wait(act, x1_ready, tile_no(m, p, -1) + 1)
                        high(x1_16[:, 0], x1T[q1][:].rearrange("p k t b -> p k (t b)"), tile_s[q1][:, 1:2])\
                            .then_inc(x1_hi_ready, 1)
                    if i == -1 and s == 0:
                        load_x(0, 0)
                    if i == 1 and s < 2:
                        wx3_high(2 + s)
                    if has[2] and s == 1:
                        wait(act, x3_ready, tile_no(m, p, 1) + 1)
                        nc.scalar.copy(x3_hi[:], x3T[q1].rearrange("p k t b -> p k (t b)")).then_inc(x3_hi_ready, 1)

            pipeline(act, iteration, prepare, second_setup)

        @block.vector
        def _(dve):
            links = [0]

            def link(ins):
                links[0] += 1
                ins.then_inc(dve_set, 1)
                dve.wait_ge(dve_set, links[0])

            def exponents(out_, in_):
                return nc.vector.tensor_scalar(out_.bitcast(i32), in_.bitcast(i32), 0x7F800000, None, ALU.bitwise_and)

            def over_power(out_, in_, top):
                return nc.vector.tensor_scalar(out_.bitcast(i32), in_.bitcast(i32), -1.0, float((127 + 127 + top) << 23),
                                               ALU.mult, ALU.add)

            def low(out_, in_, scale, hi):
                return nc.vector.scalar_tensor_tensor(out_, in_, scale, hi, ALU.mult, ALU.subtract)

            def magnitude(column, x):
                return nc.vector.tensor_reduce(absmax[:, column:column + 1], x, AX.X, ALU.max, apply_absolute_value=True)

            dve.wait_ge(ld_cond, 80)
            nc.vector.tensor_scalar(ysT[:], condT_sb[:], float(D) ** -0.5, None, ALU.mult).then_inc(ys_ready, 1)
            magnitude(0, condT_sb[:].rearrange("p k b -> p (k b)"))
            link(nc.vector.bn_stats(stats, ln_rows[:, 0]))
            link(nc.vector.bn_aggr(moments, stats))
            nc.vector.tensor_scalar(ln_s[:, 0:1], moments[:, 1:2], LN_EPS, None, ALU.add).then_inc(ln_var_ready, 1)
            dve.wait_ge(ys_ready, 1)
            nc.vector.tensor_tensor(ysq, ysT[:], ysT[:], ALU.mult)
            dve.wait_ge(ln_root_ready, 1)
            link(nc.vector.reciprocal(ln_s[:, 1:2], ln_s[:, 1:2]))
            link(nc.vector.tensor_tensor(ln_s[:, 2:3], ln_s[:, 1:2], ln_s[:, 1:2], ALU.mult))
            link(nc.vector.tensor_tensor(ln_s[:, 2:3], ln_s[:, 2:3], ln_s[:, 0:1], ALU.mult))
            link(nc.vector.tensor_scalar(ln_s[:, 2:3], ln_s[:, 2:3], -0.5, 1.5, ALU.mult, ALU.add))
            link(nc.vector.tensor_tensor(ln_s[:, 3:4], ln_s[:, 2:3], ln_s[:, 1:2], ALU.mult))
            link(nc.vector.tensor_scalar(ae, ln_rows[:, 0], moments[:, 0:1], ln_s[:, 3:4], ALU.subtract, ALU.mult))
            link(nc.vector.tensor_tensor(ae, ae, ln_rows[:, 1], ALU.mult))
            nc.vector.tensor_tensor(ae, ae, ln_rows[:, 2], ALU.add).then_inc(ae_ready, 1)
            dve.wait_ge(aeT_ps, 1)
            nc.vector.tensor_copy(aeT, ps_z[:, 0:P].rearrange("p (k b) -> p k b", b=B)).then_inc(aeT_ready, 1)
            dve.wait_ge(ld_w0, 16)
            nc.vector.tensor_tensor(w0_sq[:].rearrange("p k n -> p (k n)"), shared[:, W0_SLOT], shared[:, W0_SLOT], ALU.mult)\
              .then_inc(ys_ready, 1)
            magnitude(1, shared[:, W0_SLOT])
            dve.wait_ge(ld_x[0], 16)
            nc.vector.tensor_reduce(m_part[:], xT_sb[0][:].rearrange("p k t b -> p (k t b)"), AX.X, ALU.max,
                                    apply_absolute_value=True).then_inc(m_ready, 1)
            dve.wait_ge(ld_wx1, 16)
            magnitude(2, shared[:, WX1_SLOT])
            dve.wait_ge(u_ps, 1)
            nc.vector.tensor_tensor(hyperT, ps_x3[:, 0:P].rearrange("p (k b) -> p k b", b=B),
                                    hb1T_sb[:].unsqueeze(2).broadcast_to([P, KC, B]), ALU.add).then_inc(u_ready, 1)
            dve.wait_ge(ld_wh1, 16)
            magnitude(3, shared[:, WH1_SLOT]).then_inc(absmax_ready, 1)
            nc.vector.memset(m_least[:, 0:2], LEAST)
            nc.vector.memset(m_least[:, 2:3], 1.0)
            nc.vector.memset(m_shift[:, 1:2], 2.0 ** -X1_SHIFT)
            nc.vector.memset(m_shift[:, 2:3], 2.0 ** -X2_SHIFT)
            dve.wait_ge(dsum_ready, 1)
            nc.vector.tensor_scalar(var_d, ps_z[:, 0:P].rearrange("p (k b) -> p k b", b=B), L0_EPS, None, ALU.add)\
              .then_inc(d_var_ready, 1)

            dve.wait_ge(absmax_spread, 1)
            nc.vector.tensor_scalar(exps[:, 8:9], absmax_all[:, 0:1], 1.0, None, ALU.max)
            link(nc.vector.tensor_scalar(exps[:, 0:4], absmax_all[:, 0:4], LEAST, None, ALU.max))
            exponents(exps[:, 8:9], exps[:, 8:9])
            link(exponents(exps[:, 0:4], exps[:, 0:4]))
            over_power(scales[:, 0:4], exps[:, 0:4], TOP)
            over_power(scales[:, 8:9], exps[:, 8:9], TOP).then_inc(scales_ready, 1)
            dve.wait_ge(d_root_ready, 1)
            link(nc.vector.reciprocal(root_d, root_d))
            link(nc.vector.tensor_tensor(newton_d, root_d, root_d, ALU.mult))
            link(nc.vector.tensor_tensor(newton_d, newton_d, var_d, ALU.mult))
            link(nc.vector.tensor_scalar(newton_d, newton_d, -0.5, 1.5, ALU.mult, ALU.add))
            nc.vector.tensor_tensor(dT[:], newton_d, root_d, ALU.mult)
            dve.wait_ge(scales_ready, 1)
            nc.vector.tensor_scalar(m_shift[:, 0:1], scales[:, 0:1], 2.0 ** -(TOP - 3), None, ALU.mult)
            nc.vector.tensor_copy(tile_w[:, 0:1], s_w0)
            nc.vector.tensor_copy(tile_w[:, 1:2], s_wx1)
            link(nc.vector.tensor_tensor(unscales[:, 0:1], s_wh1, s_h, ALU.mult))
            link(over_power(unscales[:, 0:1], unscales[:, 0:1], 0))

            def weight_low(n, w_lo, w_hi, slot, s_w):
                dve.wait_ge(w_hi_ready, n + 1)
                low(w_lo[:].rearrange("p k n -> p (k n)"), shared[:, slot], s_w, w_hi[:].rearrange("p k n -> p (k n)"))\
                    .then_inc(w_lo_ready, 1)

            weight_low(0, w0_lo, w0_hi, W0_SLOT, s_w0)
            dve.wait_ge(ld_b1, 16)
            dve.wait_ge(consts_ready, 2 + RANK)

            def wx3_low(k):
                dve.wait_ge(wx3_hi_ready, k + 1)
                dve.wait_ge(w2_used, 2 * RANK)
                nc.vector.tensor_tensor(wx3_lo[:, k], shared[:, WX3_SLOT[k]], wx3_hi[:, k].bitcast(fp32), ALU.subtract)\
                  .then_inc(wx3_lo_ready[k], 1)

            def low_rank(q):
                dve.wait_ge(w2_used, RH * (q + 1))
                nc.vector.tensor_tensor(rows[:, q], ps_rows[q][:], b2_bc[:, q], ALU.add).then_inc(rows_ready, 1)

            def lstm_weight_low(k):
                dve.wait_ge(wh3_hi_ready, k + 1)
                low(wh3_lo[:, k], wh3_staged[:, k], s_wh3, wh3_hi[:, k]).then_inc(wh3_lo_ready, 1)

            def second_setup():
                magnitude(6, b_rows.rearrange("p h n -> p (h n)"))
                dve.wait_ge(absmax_spread, 2)
                link(nc.vector.tensor_reduce(exps[:, 7:8], absmax_all[:, 7:11], AX.X, ALU.max))
                link(nc.vector.tensor_scalar(exps[:, 7:8], exps[:, 7:8], LEAST, None, ALU.max))
                link(exponents(exps[:, 7:8], exps[:, 7:8]))
                over_power(s_wh3, exps[:, 7:8], TOP).then_inc(scales_ready, 1)
                dve.wait_ge(scales_ready, 2)
                link(nc.vector.tensor_tensor(unscales[:, 1:2], s_wh3, s_h, ALU.mult))
                link(over_power(unscales[:, 1:2], unscales[:, 1:2], 0))
                dve.wait_ge(ld_base, 16)
                magnitude(4, late[:])
                lstm_weight_low(0)
                lstm_weight_low(1)
                dve.wait_ge(b_moved, 16 * 2 * RANK)

            def l2_weights():
                low_rank(2)
                low_rank(3)
                dve.wait_ge(rows_ready, 4)
                magnitude(5, a_rows.rearrange("p h n -> p (h n)")).then_inc(absmax_ready, 1)
                wx3_low(0)
                dve.wait_ge(absmax_spread, 3)
                link(nc.vector.tensor_scalar(exps[:, 4:7], absmax_all[:, 4:7], LEAST, None, ALU.max))
                link(exponents(exps[:, 4:7], exps[:, 4:7]))
                link(over_power(scales[:, 4:7], exps[:, 4:7], TOP))
                link(nc.vector.tensor_scalar(l2_scales[:, 2:3], s_a, 2.0 ** -Z_SHIFT, None, ALU.mult))
                link(nc.vector.tensor_tensor(l2_scales[:, 3:4], l2_scales[:, 2:3], scales[:, 6:7], ALU.mult))
                link(nc.vector.tensor_tensor(s_base, l2_scales[:, 3:4], scales[:, 4:5], ALU.min))
                link(over_power(l2_scales[:, 2:3], l2_scales[:, 2:3], 0))
                nc.vector.tensor_tensor(s_b, l2_scales[:, 2:3], s_base, ALU.mult).then_inc(scales_ready, 1)
                x2_unscale(0)
                for n in range(2):
                    dve.wait_ge(l2_hi_ready, 2 + 2 * n)
                    for half in range(2):
                        low(a_part(a_lo, n, half), a_turned(n, half), s_a, a_part(a_hi, n, half)).then_inc(l2_lo_ready, 1)
                dve.wait_ge(l2_hi_ready, 5)
                low(b_lo[:], b_halves, s_b, b_hi[:]).then_inc(l2_lo_ready, 1)
                dve.wait_ge(l2_hi_ready, 6)
                low(base_lo[:].rearrange("p k n -> p (k n)"), late[:], s_base, base_hi[:].rearrange("p k n -> p (k n)"))\
                    .then_inc(l2_lo_ready, 1)
                dve.wait_ge(l2_lo_ready, 6)

            def x2_unscale(a):
                if isinstance(a, int) and a == 0:
                    dve.wait_ge(scales_ready, 3)
                nc.vector.tensor_tensor(x2_s[:, 1:2], x2_s[:, 0:1], s_base, ALU.mult).then_inc(x2_s_chain, 1)
                wait(dve, x2_s_chain, 2 * a + 1)
                over_power(x2_s[:, 1:2], x2_s[:, 1:2], 0).then_inc(x2_s_chain, 1)

            def tile_scales(m, p, has, first=False):
                q1 = (p + 1) % 2
                if has[2]:
                    a = tile_no(m, p, 1)
                    nc.vector.tensor_copy(x2_s[:, 0:1], tile_s[q1][:, 2:3]).then_inc(x2_s_ready, 1)
                    if not first:
                        wait(dve, x2_s_ready, a + 1)
                        x2_unscale(a)
                if has[0]:
                    a = tile_no(m, p, -1)
                    wait(dve, m_spread, a + 1)
                    nc.vector.tensor_tensor(m_exp[:], m_all[:].broadcast_to([P, 3]), m_least[:], ALU.max)\
                      .then_inc(tile_s_chain, 1)
                    wait(dve, tile_s_chain, TILE_S_LINKS * a + 1)
                    exponents(m_exp[:], m_exp[:]).then_inc(tile_s_chain, 1)
                    wait(dve, tile_s_chain, TILE_S_LINKS * a + 2)
                    over_power(m_scale[:], m_exp[:], TOP).then_inc(tile_s_chain, 1)
                    wait(dve, tile_s_chain, TILE_S_LINKS * a + 3)
                    nc.vector.tensor_tensor(tile_s[q1][:, 0:3], m_scale[:], m_shift[:], ALU.mult).then_inc(tile_s_ready, 1)
                    wait(dve, tile_s_ready, a + 1)
                    nc.vector.tensor_tensor(tile_p[:], tile_s[q1][:, 0:2], tile_w[:], ALU.mult).then_inc(tile_s_chain, 1)
                    wait(dve, tile_s_chain, TILE_S_LINKS * a + 4)
                    over_power(tile_s[q1][:, 3:5], tile_p[:], 0).then_inc(tile_s_chain, 1)
                    wait(dve, tile_s_chain, TILE_S_LINKS * a + 5)
                    nc.vector.tensor_scalar(d_un[:], dT[:], tile_s[q1][:, 3:4], None, ALU.mult)

            def prepare(m, p, has, i):
                q1 = (p + 1) % 2
                if i == -1 or i == 1:
                    tile_scales(m, p, has, True)
                if has[2]:
                    wait(dve, x2_hi_ready, tile_no(m, p, 1) + 1)
                    low(x2_16[:, 1], x2T[q1][:].rearrange("p k t b -> p k (t b)"), x2_s[:, 0:1], x2_16[:, 0])\
                        .then_inc(x2_lo_ready, 1)
                if has[0]:
                    wait(dve, xs_hi_ready, tile_no(m, p, -1) + 1)
                    low(xs16[:, 1], x1T[q1][:].rearrange("p k t b -> p k (t b)"), tile_s[q1][:, 0:1], xs16[:, 0])\
                        .then_inc(xs_lo_ready, 1)

            def iteration(m, p, has, i):
                q1 = (p + 1) % 2

                def xw_evac(j):
                    a = tile_no(m, p, 1)
                    wait(dve, xw_ps, step_no(m, p, 1, j + 1))
                    nc.vector.tensor_tensor(xw_tok[:, j], ps_xw[j % 2][:], b3_bc[:, GW * j:GW * j + GW], ALU.add)\
                      .then_inc(xw_ready, 1)

                if i == 0:
                    dve.wait_ge(ld_b2, 16 * 4 * RH)
                    low_rank(0)
                    low_rank(1)
                    dve.wait_ge(rows_ready, 2)
                if i == -1:
                    weight_low(1, wx1_lo, wx1_hi, WX1_SLOT, s_wx1)
                    weight_low(2, wh1_lo, wh1_hi, WH1_SLOT, s_wh1)
                    dve.wait_ge(h0_hi, 2)
                    low(rnn_h16[:, :, 1], condT_sb[:], s_h, rnn_h16[:, :, 0]).then_inc(h0_lo, 1)
                    low(lstm_h16[:, 1], condT_sb[:], s_h, lstm_h16[:, 0]).then_inc(h0_lo, 1)
                for s in range(STEPS):
                    t, r = step_no(m, p, 2, s), step_no(m, p, 0, s)
                    gates = xw_step[p][:, s]
                    if has[3]:
                        wait(dve, gates_ps, t + 1)
                        if s == 0:
                            wait(dve, xw_moved_first[p], FIRST_MOVES * (turn(m, p, 2) + 1))
                        if s == 1:
                            wait(dve, xw_moved[p], MOVES * (turn(m, p, 2) + 1))
                        for half in (slice(0, 2 * P), slice(2 * P, GW)):
                            nc.vector.scalar_tensor_tensor(gates[:, half], ps_gates[:, half], un_lstm, gates[:, half],
                                                           ALU.mult, ALU.add).then_inc(gates_ready, 1)
                    if has[1]:
                        wait(dve, rnn_ps, r + 1)
                        if s == 0:
                            wait(dve, xw1_ready, tile_no(m, p, 0) + 1)
                        sums = ps_rnn[:, 0:2 * P].rearrange("p (k h b) -> p k h b", h=2, b=B)
                        nc.vector.scalar_tensor_tensor(rnn_half[:], sums[:, :, 1], un_rnn, xw1T[:, :, s],
                                                       ALU.mult, ALU.add).then_inc(rnn_half_ready, 1)
                        wait(dve, rnn_half_ready, r + 1)
                        nc.vector.scalar_tensor_tensor(rnn_pre[:], sums[:, :, 0], un_rnn, rnn_half[:],
                                                       ALU.mult, ALU.add).then_inc(rnn_pre_ready, 1)
                    if has[3]:
                        wait(dve, gates_acted, 3 * t + 2)
                        nc.vector.tensor_tensor(kept, gates[:, P:2 * P], cell[:], ALU.mult)
                        nc.vector.tensor_tensor(added[:], gates[:, 0:P], gates[:, 3 * P:GW], ALU.mult)\
                          .then_inc(added_ready, 1)
                        wait(dve, added_ready, t + 1)
                        nc.vector.tensor_tensor(cell[:], kept, added[:], ALU.add).then_inc(cell_ready, 1)
                    if has[1]:
                        wait(dve, rnn_hi_ready, r + 1)
                        nc.vector.scalar_tensor_tensor(rnn_h16[:, :, 1], rnn_h[:], s_h, rnn_h16[:, :, 0],
                                                       ALU.mult, ALU.subtract).then_inc(rnn_lo_ready, 1)
                        nc.vector.tensor_tensor(x2T[p][:, :, s], x1T[p][:, :, s], rnn_h[:], ALU.add).then_inc(x2_ready, 1)
                    if has[3]:
                        wait(dve, gates_acted, 3 * t + 3)
                        wait(dve, cell_tanh_ready, t + 1)
                        nc.vector.tensor_tensor(lstm_h[:], gates[:, 2 * P:3 * P], cell_tanh[:], ALU.mult)\
                          .then_inc(lstm_h_ready, 1)
                    if has[2] and s == 3:
                        xw_evac(2)
                    if has[3]:
                        wait(dve, lstm_hi_ready, t + 1)
                        hT = ps_lstm_t[:, 0:P].rearrange("p (k b) -> p k b", b=B)
                        nc.vector.scalar_tensor_tensor(lstm_h16[:, 1], hT, s_h, lstm_h16[:, 0],
                                                       ALU.mult, ALU.subtract).then_inc(lstm_lo_ready, 1)
                        nc.vector.tensor_tensor(x3T[p][:, :, s], hT, x3T[p][:, :, s], ALU.add).then_inc(out_ready, 1)
                    if i == 0:
                        dve.wait_ge(ld_wh3[s], 16)
                        last = magnitude(7 + s, wh3_staged[:, s])
                        if s == KC - 1:
                            last.then_inc(absmax_ready, 1)
                    if has[0] and s == 0:
                        a = tile_no(m, p, -1)
                        wait(dve, l0_ready, a + 1)
                        nc.vector.tensor_tensor(x1T[q1][:], ps_feat[:].rearrange("p (k t b) -> p k t b", t=STEPS, b=B),
                                                d_un[:].unsqueeze(2).broadcast_to([P, KC, STEPS, B]), ALU.mult)\
                          .then_inc(l0_scaled, 1)
                        wait(dve, l0_scaled, a + 1)
                        nc.vector.tensor_tensor(x1T[q1][:], x1T[q1][:], xT_sb[q1][:], ALU.add).then_inc(x1_ready, 1)
                    if i == 1 and s == 0:
                        lstm_weight_low(2)
                        lstm_weight_low(3)
                        l2_weights()
                    if has[2] and s == 0:
                        a = tile_no(m, p, 1)
                        wait(dve, z_ready, a + 1)
                        nc.vector.tensor_tensor(zm[:].rearrange("p h t b -> p (h t) b"),
                                                ps_z[:, 0:TOK].rearrange("p (n b) -> p n b", b=BH),
                                                same_b[:].unsqueeze(1).broadcast_to([P, 2 * STEPS, BH]), ALU.mult)\
                          .then_inc(zm_ready, 1)
                        wait(dve, zm_hi_ready, a + 1)
                        low(zm16[:, 1], zm.rearrange("p h t b -> p h (t b)"), 2.0 ** -Z_SHIFT, zm16[:, 0])\
                            .then_inc(zm_lo_ready, 1)
                    if has[0] and s == 0:
                        wait(dve, x1_hi_ready, tile_no(m, p, -1) + 1)
                        low(x1_16[:, 1], x1T[q1][:].rearrange("p k t b -> p k (t b)"), tile_s[q1][:, 1:2], x1_16[:, 0])\
                            .then_inc(x1_lo_ready, 1)
                    if has[4] and s == 1:
                        wait(dve, ld_x[p], 16 * (turn(m, p, -2) + 1))
                        wait(dve, m_spread, tile_no(m, p, -2))
                        nc.vector.tensor_reduce(m_part[:], xT_sb[p][:].rearrange("p k t b -> p (k t b)"), AX.X, ALU.max,
                                                apply_absolute_value=True).then_inc(m_ready, 1)
                    if i == 1 and s == 1:
                        wx3_low(KC - 1)
                    if has[2] and s == 1:
                        a = tile_no(m, p, 1)
                        wait(dve, x3_ps, a + 1)
                        wait(dve, x2_s_chain, 2 * a + 2)
                        wait(dve, st_out[q1], 16 * turn(m, p, 1))
                        nc.vector.scalar_tensor_tensor(x3T[q1].rearrange("p k t b -> p (k t b)"), ps_x3[:], x2_s[:, 1:2],
                                                       x2T[q1][:].rearrange("p k t b -> p (k t b)"), ALU.mult, ALU.add)\
                          .then_inc(x3_scaled, 1)
                        wait(dve, x3_scaled, a + 1)
                        nc.vector.tensor_tensor(x3T[q1], x3T[q1], x2T[q1][:], ALU.add).then_inc(x3_ready, 1)
                    if i == 1 and s == 1:
                        dve.wait_ge(ld_b3, 16)
                    if has[2] and s == 2:
                        xw_evac(0)
                    if s == 2 and i != 0 and i != TAIL[-1]:
                        tile_scales(m + p, (p + 1) % 2, [True] * 5 if i is None else stages(i + 1))
                    if has[2] and s == 2:
                        xw_evac(1)
                    if has[2] and s == 3:
                        xw_evac(3)
                    if has[0] and s == 3:
                        a = tile_no(m, p, -1)
                        wait(dve, xw1_ps, a + 1)
                        nc.vector.scalar_tensor_tensor(xw1T[:].rearrange("p k t b -> p k (t b)"),
                                                       ps_feat[:].rearrange("p (k n) -> p k n", k=KC), tile_s[q1][:, 4:5],
                                                       b1T_sb[:].unsqueeze(2).broadcast_to([P, KC, TOK]), ALU.mult, ALU.add)\
                          .then_inc(xw1_ready, 1)

            pipeline(dve, iteration, prepare, second_setup)

        @block.tensor
        def _(pe):
            pe.wait_ge(consts_ready, 2 + RANK)
            pe.wait_ge(ae_ready, 1)
            for k in range(KC):
                last = nc.tensor.transpose(ps_z[:, B * k:B * k + B], ae[:, P * k:P * k + P], ident[0:B, 0:B])
            last.then_inc(aeT_ps, 1)
            pe.wait_ge(ld_w1, 16)
            pe.wait_ge(aeT_ready, 1)
            for oc in range(KC):
                for k in range(KC):
                    last = nc.tensor.matmul(ps_x3[:, B * oc:B * oc + B], w1_sb[:, k, P * oc:P * oc + P], aeT[:, k],
                                            start=(k == 0), stop=(k == KC - 1))
            last.then_inc(u_ps, 1)
            pe.wait_ge(ys_ready, 2)
            for oc in range(KC):
                for k in range(KC):
                    last = nc.tensor.matmul(ps_z[:, B * oc:B * oc + B], w0_sq[:, k, P * oc:P * oc + P], ysq[:, k],
                                            start=(k == 0), stop=(k == KC - 1))
            last.then_inc(dsum_ready, 1)
            pe.wait_ge(hyper_ready, 1)

            def w2_piece(n):
                q, j = n // RH, n % RH
                pe.wait_ge(ld_ring[n % RING], 16 * (n // RING + 1))
                for k in range(KC):
                    last = nc.tensor.matmul(ps_rows[q][B * j:B * j + B, :], hyperT[:, k], ring[:, n % RING, k],
                                            start=(k == 0), stop=(k == KC - 1), tile_position=(0, B * j))
                last.then_inc(w2_used, 1)

            w2_piece(0)
            w2_piece(1)
            W2_BETWEEN = {(-1, 0): (2, 3, 4), (-1, 1): (5, 6), (-1, 2): (7,), (0, 3): (8, 9, 10, 11)}

            def l2_weights():
                for n in range(RANK + 4, 2 * RANK):
                    w2_piece(n)
                pe.wait_ge(rows_ready, 4)
                for n in range(2):
                    for k in range(2):
                        for q in range(2):
                            at = P * (2 * k + q)
                            last = nc.tensor.transpose(ps_turned[n][:, at:at + P],
                                                       a_rows[:, q, P * (2 * n + k):P * (2 * n + k) + P], ident[:])
                    last.then_inc(a_ps, 1)

            def split_product(psum, w_parts, x_parts, first=True, final=True):
                (w_hi, w_lo), (x_hi, x_lo) = w_parts, x_parts
                triples = [(w, x) for ws, xs_ in ((w_hi, x_hi), (w_hi, x_lo), (w_lo, x_hi)) for w, x in zip(ws, xs_)]
                for n, (w, x) in enumerate(triples):
                    last = nc.tensor.matmul(psum, w, x, start=(first and n == 0), stop=(final and n == len(triples) - 1))
                return last

            def chunks(w, at):
                return [w[:, k, at:at + P] for k in range(KC)]

            def dense(psum, w_hi, w_lo, x16, outs, **flags):
                for oc in outs:
                    last = split_product(psum[:, TOK * oc:TOK * oc + TOK], (chunks(w_hi, P * oc), chunks(w_lo, P * oc)),
                                         [[x16[:, part, k] for k in range(KC)] for part in range(2)], **flags)
                return last

            def of_half(x, half):
                return x.rearrange("p (t b) -> p t b", t=STEPS)[:, :, BH * half:BH * half + BH]

            def z(half):
                return split_product(ps_z[:, ZN * half:ZN * half + ZN],
                                     [[w[:, half, k] for k in range(KC)] for w in (a_hi, a_lo)],
                                     [[of_half(x2_16[:, part, k], half) for k in range(KC)] for part in range(2)])

            def x3_base(outs):
                for oc in outs:
                    last = dense(ps_x3, base_hi, base_lo, x2_16, (oc,), first=(oc == 0), final=False)
                return last

            def x3_low_rank(outs):
                for oc in outs:
                    for half in range(2):
                        last = split_product(of_half(ps_x3[:, TOK * oc:TOK * oc + TOK], half),
                                             [[w[:, half, P * oc:P * oc + P]] for w in (b_hi, b_lo)],
                                             [[zm16[:, part, half]] for part in range(2)], first=False, final=(oc == KC - 1 and half == 1))
                return last

            XW_PARTS = [(x, w, k) for x, w in ((x3_hi, wx3_hi), (x3_hi, wx3_lo), (x3_lo, wx3_hi)) for k in range(KC)]

            def xw(j, begin=0, end=len(XW_PARTS)):
                for n in range(begin, end):
                    x, w, k = XW_PARTS[n]
                    last = nc.tensor.matmul(ps_xw[j % 2][:], x[:, k], w[:, k, GW * j:GW * j + GW],
                                            start=(n == 0), stop=(n == len(XW_PARTS) - 1))
                return last

            def lstm_product():
                parts = [(0, wh3_hi), (0, wh3_lo), (1, wh3_hi)]
                for n, (part, w) in enumerate(parts):
                    for k in range(KC):
                        for j in range(KC):
                            last = nc.tensor.matmul(ps_gates[B * j:B * j + B, :], lstm_h16[:, part, k],
                                                    w[:, k, GW * j:GW * j + GW], start=(n == 0 and k == 0),
                                                    stop=(n == 2 and k == KC - 1), tile_position=(0, B * j))
                return last

            def rnn_product():
                for oc in range(KC):
                    at = 2 * B * oc
                    for k in range(KC):
                        nc.tensor.matmul(ps_rnn[:, at:at + 2 * B], wh1_hi[:, k, P * oc:P * oc + P],
                                         rnn_h16[:, k].rearrange("p h b -> p (h b)"), start=(k == 0), stop=False)
                    for k in range(KC):
                        last = nc.tensor.matmul(ps_rnn[:, at:at + B], wh1_lo[:, k, P * oc:P * oc + P], rnn_h16[:, k, 0],
                                                start=False, stop=(k == KC - 1))
                return last

            def iteration(m, p, has, i):
                q1 = (p + 1) % 2
                if i == -1:
                    pe.wait_ge(w_lo_ready, 1)
                if i == 0:
                    pe.wait_ge(h0_lo, 2)
                    pe.wait_ge(w_lo_ready, 3)
                for s in range(STEPS):
                    t, r = step_no(m, p, 2, s), step_no(m, p, 0, s)
                    if has[3]:
                        wait(pe, lstm_lo_ready, t)
                        lstm_product().then_inc(gates_ps, 1)
                    if has[1]:
                        wait(pe, rnn_lo_ready, r)
                        rnn_product().then_inc(rnn_ps, 1)
                    if s == 0 and has[0]:
                        wait(pe, xs_lo_ready, tile_no(m, p, -1) + 1)
                        wait(pe, xw1_ready, tile_no(m, p, 0) + 1 if has[1] else 0)
                        dense(ps_feat, w0_hi, w0_lo, xs16, range(KC)).then_inc(l0_ready, 1)
                    if i == 1 and s == 0:
                        l2_weights()
                        pe.wait_ge(l2_lo_ready, 4)
                    if s == 0 and has[2]:
                        wait(pe, x2_lo_ready, tile_no(m, p, 1) + 1)
                        z(0)
                    if s == 1 and has[2]:
                        x3_base((2, 3))
                        wait(pe, zm_lo_ready, tile_no(m, p, 1) + 1)
                        x3_low_rank(range(KC)).then_inc(x3_ps, 1)
                    if s == 1 and has[0]:
                        wait(pe, x1_lo_ready, tile_no(m, p, -1) + 1)
                        wait(pe, w_lo_ready, 2 if i == -1 else 0)
                        dense(ps_feat, wx1_hi, wx1_lo, x1_16, (0, 1))
                    if i == 1 and s == 2:
                        for k in range(KC):
                            pe.wait_ge(wx3_lo_ready[k], 1)
                        pe.wait_ge(wh3_lo_ready, KC)
                    if s == 2 and has[2]:
                        wait(pe, x3_lo_ready, tile_no(m, p, 1) + 1)
                    if s >= 2 and has[2]:
                        wait(pe, xw_ready, step_no(m, p, 1, 0) + 2 * (s - 2) - 1)
                        xw(2 * (s - 2)).then_inc(xw_ps, 1)
                    if s == 3 and has[2]:
                        wait(pe, xw_ready, step_no(m, p, 1, 2))
                        xw(3, 0, 6)
                    if has[3]:
                        wait(pe, lstm_h_ready, t + 1)
                        nc.tensor.transpose(ps_lstm_t[:, 0:P], lstm_h[:], ident[:]).then_inc(lstm_t_ps, 1)
                    if s == 0 and has[2]:
                        z(1).then_inc(z_ready, 1)
                        wait(pe, l2_lo_ready, 6 if i == 1 else 0)
                        x3_base((0, 1))
                    if s == 1 and has[0]:
                        dense(ps_feat, wx1_hi, wx1_lo, x1_16, (2, 3)).then_inc(xw1_ps, 1)
                    if s == 2 and has[2]:
                        wait(pe, xw_ready, step_no(m, p, 1, 0))
                        xw(1).then_inc(xw_ps, 1)
                    if s == 3 and has[2]:
                        xw(3, 6).then_inc(xw_ps, 1)
                    for n in W2_BETWEEN.get((i, s), ()):
                        w2_piece(n)

            pipeline(pe, iteration)


def kernel(**inputs):
    import numpy as np
    import concourse.bacc as bacc
    from concourse.bass_utils import run_bass_kernel_spmd

    a = {k: np.asarray(v) for k, v in inputs.items()}
    feature_major = (TILES, STEPS, B, KC, P)

    def gates_by_chunk(w):
        return w.reshape(-1, GATES, KC, P).transpose(0, 2, 1, 3).reshape(w.shape[0] if w.ndim > 1 else KC, -1)

    arrays = {
        "xT": a["x"].transpose(1, 0, 2).reshape(feature_major).transpose(0, 4, 3, 1, 2),
        "condT": a["cond_1024"].reshape(B, KC, P).transpose(2, 1, 0),
        "cond": a["cond_1024"],
        "w0": a["L0_cond_weight"],
        "wx1": a["L1_cond_Wx"], "wh1": a["L1_cond_Wh"], "b1T": a["L1_cond_b"].reshape(KC, P).T,
        "base": a["L2_cond_base_layer"],
        "hw1": a["L2_cond_w1"], "hb1T": a["L2_cond_b1"].reshape(KC, P).T,
        "hw2": a["L2_cond_w2"].reshape(-1, 2, D, RANK).transpose(1, 3, 0, 2),
        "hb2": a["L2_cond_b2"].reshape(2, D, RANK).transpose(0, 2, 1),
        "ln_g": a["L2_cond_ln_g"], "ln_b": a["L2_cond_ln_b"],
        "wx3": gates_by_chunk(a["L3_cond_Wx"]), "wh3": gates_by_chunk(a["L3_cond_Wh"]),
        "b3": gates_by_chunk(a["L3_cond_b"]),
    }
    nc = bacc.Bacc("TRN2", target_bir_lowering=False, num_devices=1)
    fed, args = {}, []
    for name, v in arrays.items():
        v = np.ascontiguousarray(v)
        fed[f"in_{name}"] = v
        args.append(nc.dram_tensor(f"in_{name}", v.shape, mybir.dt.from_np(v.dtype), kind="ExternalInput").ap())
    out = nc.dram_tensor("outT", (TILES, P, KC, STEPS, B), mybir.dt.float32, kind="ExternalOutput").ap()
    build(nc, *args, out)
    r = run_bass_kernel_spmd(nc, [fed], core_ids=[0])
    got = r.results[0]["outT"]
    return got.transpose(4, 0, 3, 2, 1).reshape(B, T, D)
```
